# Optimizing a Trainium2 kernel written in Bass

```python
import numpy as np
import jax
import jax.numpy as jnp

def _softmax(x, axis=-1):
    return jax.nn.softmax(x, axis=axis)

def _gelu(x):
    return jax.nn.gelu(x, approximate=True)

def _silu(x):
    return jax.nn.silu(x)

def _sigmoid(x):
    return jax.nn.sigmoid(x)

def _layernorm(x, axis=-1, eps=1e-05):
    m = jnp.mean(x, axis=axis, keepdims=True)
    v = jnp.var(x, axis=axis, keepdims=True)
    return (x - m) / jnp.sqrt(v + eps)

def _scatter_add(tgt, idx, src, axis=0):
    return tgt.at[idx].add(src)

def _segment_sum(src, seg, n):
    return jax.ops.segment_sum(src, seg, n)
kernel_name = 'mk_vit_tower_d2_tok_img1024_r4_cc9b58'

def setup_inputs(seed: int=0):
    np.random.seed(seed)
    _w = jnp.asarray

    def _rec_inputs():
        import jax
        import jax.numpy as jnp
        _rk = jax.random.key(seed)
        x = -0.000222058 + 0.999998 * jax.random.normal(jax.random.fold_in(_rk, 1), (128, 3, 64, 64), jnp.float32)
        return x
    x = _rec_inputs()

    def _L0_tok_setup():
        import jax, jax.numpy as jnp
        import numpy as np
        IMG, PS, C, OUT = (64, 16, 3, 256)
        NP = IMG // PS
        IN_FEAT = C * PS * PS
        key = jax.random.key(seed)
        k1, k2, k3, k4 = jax.random.split(key, 4)
        x = jax.random.normal(k1, (128, C, IMG, IMG), dtype=jnp.float32)
        W = jax.random.normal(k2, (OUT, IN_FEAT), dtype=jnp.float32) / np.sqrt(IN_FEAT)
        b = jax.random.normal(k3, (OUT,), dtype=jnp.float32) * 0.01
        pos_emb = jax.random.normal(k4, (NP * NP, OUT), dtype=jnp.float32)
        return {'x': x, 'W': W, 'b': b, 'pos_emb': pos_emb}
    _L0_tok_all = _L0_tok_setup()
    _L0_tok_in = {k: v for k, v in _L0_tok_all.items() if k in ('W', 'b', 'pos_emb')}
    del _L0_tok_all

    def _L0_attn_setup():
        import jax, jax.numpy as jnp
        import numpy as np
        N_HEADS = 16

        def _alibi_causal_mask(T, n_heads, dtype):
            slopes = (1.0 / jnp.power(2.0, jnp.arange(1, n_heads + 1, dtype=dtype)))[:, None, None]
            idx = jnp.arange(T)
            rel = (idx[None, :] - idx[:, None]).astype(dtype)
            alibi = jnp.tril(rel)
            causal = jnp.where(idx[None, :] > idx[:, None], -jnp.inf, 0.0).astype(dtype)
            return (alibi + causal)[None, :, :] * slopes
        key = jax.random.key(seed)
        ks = jax.random.split(key, 5)
        B, T, C = (2, 512, 256)
        scale = 0.02
        return {'x': jax.random.normal(ks[0], (B, T, C), dtype=jnp.float32), 'W_attn': jax.random.normal(ks[1], (C, 3 * C), dtype=jnp.float32) * scale, 'b_attn': jax.random.normal(ks[2], (3 * C,), dtype=jnp.float32) * scale, 'W_proj': jax.random.normal(ks[3], (C, C), dtype=jnp.float32) * scale, 'b_proj': jax.random.normal(ks[4], (C,), dtype=jnp.float32) * scale}
    _L0_attn_all = _L0_attn_setup()
    _L0_attn_in = {k: v for k, v in _L0_attn_all.items() if k in ('W_attn', 'b_attn', 'W_proj', 'b_proj')}
    del _L0_attn_all

    def _L0_ffn_setup():
        import jax, jax.numpy as jnp
        import numpy as np
        E, TOP_K, D, H = (8, 2, 256, 512)
        B, S = (2, 512)
        key = jax.random.key(seed)
        ks = jax.random.split(key, 10)
        s = 0.02
        return {'x': jax.random.normal(ks[0], (B, S, D), dtype=jnp.float32), 'gate_w': jax.random.normal(ks[1], (E, D), dtype=jnp.float32) * s, 'gate_b': jnp.zeros((E,), dtype=jnp.float32), 'w0': jax.random.normal(ks[2], (E, H, D), dtype=jnp.float32) * s, 'b0': jnp.zeros((E, H), dtype=jnp.float32), 'w1': jax.random.normal(ks[3], (E, H, D), dtype=jnp.float32) * s, 'b1': jnp.zeros((E, H), dtype=jnp.float32), 'w2': jax.random.normal(ks[4], (E, D, H), dtype=jnp.float32) * s, 'b2': jnp.zeros((E, D), dtype=jnp.float32)}
    _L0_ffn_all = _L0_ffn_setup()
    _L0_ffn_in = {k: v for k, v in _L0_ffn_all.items() if k in ('gate_w', 'gate_b', 'w0', 'b0', 'w1', 'b1', 'w2', 'b2')}
    del _L0_ffn_all

    def _L1_attn_setup():
        import jax, jax.numpy as jnp
        import numpy as np
        import math
        N_HEADS = 16
        ROPE_BASE = 10000.0

        def _rope_interleaved(t, cos, sin):
            te, to = (t[..., 0::2], t[..., 1::2])
            re = te * cos - to * sin
            ro = te * sin + to * cos
            return jnp.stack([re, ro], axis=-1).reshape(t.shape)
        key = jax.random.key(seed)
        ks = jax.random.split(key, 5)
        B, T, C = (2, 512, 256)
        s = 1.0 / math.sqrt(C)
        return {'x': jax.random.normal(ks[0], (B, T, C), dtype=jnp.float32), 'W_qkv': jax.random.normal(ks[1], (C, 3 * C), dtype=jnp.float32) * s, 'b_qkv': jax.random.normal(ks[2], (3 * C,), dtype=jnp.float32) * 0.02, 'W_proj': jax.random.normal(ks[3], (C, C), dtype=jnp.float32) * s, 'b_proj': jax.random.normal(ks[4], (C,), dtype=jnp.float32) * 0.02}
    _L1_attn_all = _L1_attn_setup()
    _L1_attn_in = {k: v for k, v in _L1_attn_all.items() if k in ('W_qkv', 'b_qkv', 'W_proj', 'b_proj')}
    del _L1_attn_all

    def _L1_ffn_setup():
        import jax, jax.numpy as jnp
        import numpy as np
        NUM_EXPERTS_TOTAL = 9
        TOP_K = 2
        key = jax.random.key(seed)
        k0, k1, k2, k3, k4 = jax.random.split(key, 5)
        B, S, H, I = (2, 512, 256, 704)
        E = NUM_EXPERTS_TOTAL
        x = jax.random.normal(k0, (B, S, H), dtype=jnp.float32)
        Wr = jax.random.normal(k1, (H, E), dtype=jnp.float32) * 0.02
        Wg = jax.random.normal(k2, (E, H, I), dtype=jnp.float32) * 0.02
        Wu = jax.random.normal(k3, (E, H, I), dtype=jnp.float32) * 0.02
        Wd = jax.random.normal(k4, (E, I, H), dtype=jnp.float32) * 0.02
        return {'x': x, 'Wr': Wr, 'Wg': Wg, 'Wu': Wu, 'Wd': Wd}
    _L1_ffn_all = _L1_ffn_setup()
    _L1_ffn_in = {k: v for k, v in _L1_ffn_all.items() if k in ('Wr', 'Wg', 'Wu', 'Wd')}
    del _L1_ffn_all
    return {'x': x, 'L0_tok_W': _L0_tok_in['W'], 'L0_tok_b': _L0_tok_in['b'], 'L0_tok_pos_emb': _L0_tok_in['pos_emb'], 'L0_attn_W_attn': _L0_attn_in['W_attn'], 'L0_attn_b_attn': _L0_attn_in['b_attn'], 'L0_attn_W_proj': _L0_attn_in['W_proj'], 'L0_attn_b_proj': _L0_attn_in['b_proj'], 'L0_ffn_gate_w': _L0_ffn_in['gate_w'], 'L0_ffn_gate_b': _L0_ffn_in['gate_b'], 'L0_ffn_w0': _L0_ffn_in['w0'], 'L0_ffn_b0': _L0_ffn_in['b0'], 'L0_ffn_w1': _L0_ffn_in['w1'], 'L0_ffn_b1': _L0_ffn_in['b1'], 'L0_ffn_w2': _L0_ffn_in['w2'], 'L0_ffn_b2': _L0_ffn_in['b2'], 'L1_attn_W_qkv': _L1_attn_in['W_qkv'], 'L1_attn_b_qkv': _L1_attn_in['b_qkv'], 'L1_attn_W_proj': _L1_attn_in['W_proj'], 'L1_attn_b_proj': _L1_attn_in['b_proj'], 'L1_ffn_Wr': _L1_ffn_in['Wr'], 'L1_ffn_Wg': _L1_ffn_in['Wg'], 'L1_ffn_Wu': _L1_ffn_in['Wu'], 'L1_ffn_Wd': _L1_ffn_in['Wd']}

def reference(x, L0_tok_W, L0_tok_b, L0_tok_pos_emb, L0_attn_W_attn, L0_attn_b_attn, L0_attn_W_proj, L0_attn_b_proj, L0_ffn_gate_w, L0_ffn_gate_b, L0_ffn_w0, L0_ffn_b0, L0_ffn_w1, L0_ffn_b1, L0_ffn_w2, L0_ffn_b2, L1_attn_W_qkv, L1_attn_b_qkv, L1_attn_W_proj, L1_attn_b_proj, L1_ffn_Wr, L1_ffn_Wg, L1_ffn_Wu, L1_ffn_Wd):
    import jax
    import jax.numpy as jnp

    def _L0_tok_ref(x, W, b, pos_emb):
        import jax, jax.numpy as jnp
        import numpy as np
        IMG, PS, C, OUT = (64, 16, 3, 256)
        NP = IMG // PS
        IN_FEAT = C * PS * PS
        B = x.shape[0]
        p = x.reshape(B, C, NP, PS, NP, PS).transpose(0, 1, 2, 4, 3, 5)
        p = p.transpose(0, 2, 3, 1, 4, 5)
        p = p.reshape(B, NP * NP, IN_FEAT)
        out = jnp.einsum('bnf,of->bno', p, W) + b + pos_emb
        return out

    def _L0_attn_ref(x, W_attn, b_attn, W_proj, b_proj):
        import jax, jax.numpy as jnp
        import numpy as np
        N_HEADS = 16

        def _alibi_causal_mask(T, n_heads, dtype):
            slopes = (1.0 / jnp.power(2.0, jnp.arange(1, n_heads + 1, dtype=dtype)))[:, None, None]
            idx = jnp.arange(T)
            rel = (idx[None, :] - idx[:, None]).astype(dtype)
            alibi = jnp.tril(rel)
            causal = jnp.where(idx[None, :] > idx[:, None], -jnp.inf, 0.0).astype(dtype)
            return (alibi + causal)[None, :, :] * slopes
        B, T, C = x.shape
        H = N_HEADS
        D = C // H
        qkv = x @ W_attn + b_attn
        q, k, v = jnp.split(qkv, 3, axis=-1)
        q = q.reshape(B, T, H, D).transpose(0, 2, 1, 3)
        k = k.reshape(B, T, H, D).transpose(0, 2, 1, 3)
        v = v.reshape(B, T, H, D).transpose(0, 2, 1, 3)
        att = jnp.einsum('bhtd,bhsd->bhts', q, k) / jnp.sqrt(jnp.asarray(D, x.dtype))
        att = att + _alibi_causal_mask(T, H, x.dtype)[None]
        att = jax.nn.softmax(att, axis=-1)
        y = jnp.einsum('bhts,bhsd->bhtd', att, v)
        y = y.transpose(0, 2, 1, 3).reshape(B, T, C)
        return y @ W_proj + b_proj

    def _L0_ffn_ref(x, gate_w, gate_b, w0, b0, w1, b1, w2, b2):
        import jax, jax.numpy as jnp
        import numpy as np
        E, TOP_K, D, H = (8, 2, 256, 512)
        B, S = (2, 512)
        Bn, Sq, Dv = x.shape
        xt = x.reshape(-1, Dv)
        logits = xt @ gate_w.T + gate_b
        top_v, top_i = jax.lax.top_k(logits, TOP_K)
        h0 = jnp.einsum('td,ehd->eth', xt, w0) + b0[:, None, :]
        h1 = jnp.einsum('td,ehd->eth', xt, w1) + b1[:, None, :]
        act = h0 * jax.nn.silu(h1)
        out_all = jnp.einsum('eth,edh->etd', act, w2) + b2[:, None, :]
        out_te = jnp.transpose(out_all, (1, 0, 2))
        sel = jnp.take_along_axis(out_te, top_i[:, :, None], axis=1)
        w = jax.nn.softmax(top_v, axis=-1)[:, :, None]
        out = (w * sel).sum(axis=1)
        return out.reshape(Bn, Sq, Dv)

    def _L1_attn_ref(x, W_qkv, b_qkv, W_proj, b_proj):
        import jax, jax.numpy as jnp
        import numpy as np
        import math
        N_HEADS = 16
        ROPE_BASE = 10000.0

        def _rope_interleaved(t, cos, sin):
            te, to = (t[..., 0::2], t[..., 1::2])
            re = te * cos - to * sin
            ro = te * sin + to * cos
            return jnp.stack([re, ro], axis=-1).reshape(t.shape)
        B, T, C = x.shape
        H = N_HEADS
        dk = C // H
        qkv = x @ W_qkv + b_qkv
        q, k, v = jnp.split(qkv, 3, axis=-1)
        q = q.reshape(B, T, H, dk).transpose(0, 2, 1, 3)
        k = k.reshape(B, T, H, dk).transpose(0, 2, 1, 3)
        v = v.reshape(B, T, H, dk).transpose(0, 2, 1, 3)
        freqs = ROPE_BASE ** (-2.0 * jnp.arange(dk // 2, dtype=jnp.float32) / dk)
        angles = jnp.arange(T, dtype=jnp.float32)[:, None] * freqs[None, :]
        cos, sin = (jnp.cos(angles), jnp.sin(angles))
        q = _rope_interleaved(q, cos, sin)
        k = _rope_interleaved(k, cos, sin)
        attn = jnp.einsum('bhqd,bhkd->bhqk', q, k) / math.sqrt(dk)
        causal = jnp.triu(jnp.full((T, T), -jnp.inf, dtype=attn.dtype), k=1)
        attn = jax.nn.softmax(attn + causal, axis=-1)
        scores = jnp.einsum('bhqk,bhkd->bhqd', attn, v)
        scores = scores.transpose(0, 2, 1, 3).reshape(B, T, C)
        return scores @ W_proj + b_proj

    def _L1_ffn_ref(x, Wr, Wg, Wu, Wd):
        import jax, jax.numpy as jnp
        import numpy as np
        NUM_EXPERTS_TOTAL = 9
        TOP_K = 2
        B, S, H = x.shape
        E = NUM_EXPERTS_TOTAL
        T = B * S
        logits = jnp.einsum('bsh,he->bse', x, Wr)
        probs = jax.nn.softmax(logits, axis=-1)
        topk_w, topk_idx = jax.lax.top_k(probs, TOP_K)
        topk_w = topk_w / jnp.sum(topk_w, axis=-1, keepdims=True)
        xf = x.reshape(T, H)
        wf = topk_w.reshape(T, TOP_K)
        idxf = topk_idx.reshape(T, TOP_K)
        cw = jnp.zeros((T, E), dtype=x.dtype).at[jnp.arange(T)[:, None], idxf].add(wf)
        gate = jax.nn.silu(jnp.einsum('th,ehi->tei', xf, Wg))
        hidden = gate * jnp.einsum('th,ehi->tei', xf, Wu)
        out = jnp.einsum('tei,eih,te->th', hidden, Wd, cw)
        return out.reshape(B, S, H)
    h = _L0_tok_ref(x, L0_tok_W, L0_tok_b, L0_tok_pos_emb)
    h = h + _L0_attn_ref(_layernorm(h, axis=-1), L0_attn_W_attn, L0_attn_b_attn, L0_attn_W_proj, L0_attn_b_proj)
    h = h + _L0_ffn_ref(_layernorm(h, axis=-1), L0_ffn_gate_w, L0_ffn_gate_b, L0_ffn_w0, L0_ffn_b0, L0_ffn_w1, L0_ffn_b1, L0_ffn_w2, L0_ffn_b2)
    h = h + _L1_attn_ref(_layernorm(h, axis=-1), L1_attn_W_qkv, L1_attn_b_qkv, L1_attn_W_proj, L1_attn_b_proj)
    h = h + _L1_ffn_ref(_layernorm(h, axis=-1), L1_ffn_Wr, L1_ffn_Wg, L1_ffn_Wu, L1_ffn_Wd)
    return h

_drawn_inputs = setup_inputs


def setup_inputs(seed=0):
    import zlib

    import numpy as np

    out = dict(_drawn_inputs(seed))
    spreads = {'L0_ffn_gate_b': (0.0, 0.1),
     'L0_ffn_b0': (0.0, 0.8),
     'L0_ffn_b1': (0.0, 0.8),
     'L0_ffn_b2': (0.0, 0.1)}
    factors = {'L0_tok_b': 6.021,
     'L0_attn_b_attn': 7.862,
     'L0_attn_b_proj': 3.292,
     'L0_ffn_w0': 4.082,
     'L0_ffn_w1': 4.173,
     'L0_ffn_w2': 3.873,
     'L1_attn_b_qkv': 3.516,
     'L1_attn_b_proj': 4.506,
     'L1_ffn_Wr': 5.104,
     'L1_ffn_Wg': 4.439,
     'L1_ffn_Wu': 4.399,
     'L1_ffn_Wd': 4.408}
    for name, (base, spread) in spreads.items():
        noise = np.random.default_rng([zlib.crc32(name.encode()), seed]).standard_normal(out[name].shape)
        drawn = base * np.exp(spread * noise) if base else spread * noise
        out[name] = jnp.asarray(drawn.astype(out[name].dtype))
    for name, factor in factors.items():
        out[name] = (out[name] * factor).astype(out[name].dtype)
    return out
```

```python
from contextlib import ExitStack

import concourse.bass as bass
from concourse import mybir

F32 = mybir.dt.float32
BF16 = mybir.dt.bfloat16
I32 = mybir.dt.int32
U32 = mybir.dt.uint32
ALU = mybir.AluOpType
ACT = mybir.ActivationFunctionType
AX = mybir.AxisListType

P = 128
D = 256
KD = D // P
IMGS, NPATCH = 128, 16
TOK = IMGS * NPATCH
NT = TOK // P
IPT = P // NPATCH
NH, HD = 16, 16
HPC = P // HD
FEAT = 768
KF = FEAT // P
PAD = 48
WIN = HD + PAD
EPS = 1e-5
UNROLL = 4
LAG_RANK = 4

E = (8, 9)
HID = (512, 704)
HPAD = (512, 768)
NTILE = tuple(TOK * 2 // P + e - 1 for e in E)
JMAX = max(NTILE)
SLOT = 4352
DUMMY = TOK
ROWS = TOK + P

CONSTS = {}


def _columns():
    at = 0
    for name, n in (("ident", P), ("swap", P), ("upper", P), ("ones", P), ("cos", 16), ("sin", 16),
                    ("mask0", 32), ("mask1", 32), ("block", 8), ("tokid", NT), ("eoff", 9),
                    ("eidx", 9), ("steps", 16), ("tri", 81), ("tile", JMAX), ("nhalf", 1)):
        CONSTS[name] = (at, n)
        at += n
    return at


NCONST = _columns()


def tower(nc, a, tables, out):
    with ExitStack() as ctx:
        def sb(name, shape, dt=F32):
            return ctx.enter_context(nc.sbuf_tensor(name, shape, dt))

        def sem(name):
            return ctx.enter_context(nc.semaphore(name))

        def sem2(name):
            return [sem(f"{name}_{layer}") for layer in range(2)]

        experts = sb("experts", [P, 9 * SLOT])
        consts = sb("consts", [P, NCONST])
        w_qkv = sb("w_qkv", [P, KD, 3 * D])
        w_proj = sb("w_proj", [P, KD, D])
        bias_qk = sb("bias_qk", [P, 4])
        bias_v = sb("bias_v", [P, D])
        bias_proj = sb("bias_proj", [P, D])
        w_gate = sb("w_gate", [P, KD, 9])
        bias_gate = sb("bias_gate", [P, 8])
        h = sb("h", [P, UNROLL, D])
        xln = sb("xln", [P, D])
        xlnT = sb("xlnT", [P, KD, P])
        qk_raw = sb("qk_raw", [P, 4, P])
        rot = sb("rot", [P, 4, P])
        q_sb = sb("q_sb", [P, KD, P])
        k_sb = sb("k_sb", [P, KD, P + PAD])
        v_sb = sb("v_sb", [P, 2, D + PAD])
        spread = sb("spread", [P, 2 * 2 * IPT * P])
        qblk = spread[:, 0:2048].rearrange("p (u g n) -> p u g n", g=HPC, n=16)
        pblk = spread[:, 2048:4096].rearrange("p (g b n) -> p g b n", b=IPT, n=16)
        s_sb = sb("s_sb", [P, 2 * IPT, 16])
        p_sb = sb("p_sb", [P, 2 * IPT, 16])
        s_max = sb("s_max", [P, 2 * IPT])
        s_sum = sb("s_sum", [P, 2 * IPT])
        s_inv = sb("s_inv", [P, 2 * IPT])
        o_sb = sb("o_sb", [P, D])
        oT = sb("oT", [P, KD, P])
        xln2 = sb("xln2", [P, 2, D])
        xln2T = sb("xln2T", [P, KD, P])
        stats = sb("stats", [P, 2, 6])
        moments = sb("moments", [P, 2, 2])
        var_eps = sb("var_eps", [P, 2])
        rstd = sb("rstd", [P, 2])
        upper_bf = sb("upper_bf", [P, P], BF16)
        ones_bf = sb("ones_bf", [P, P], BF16)
        tok_id = sb("tok_id", [P, NT], I32)
        logits = sb("logits", [P, 9])
        top = sb("top", [P, 8])
        top_i = sb("top_i", [P, 8], U32)
        top_f = sb("top_f", [P, 2])
        gap = sb("gap", [P, 1])
        egap = sb("egap", [P, 1])
        wgt = sb("wgt", [P, 2])
        pick = sb("pick", [P, 2, 9])
        both_bf = sb("both_bf", [P, 9], BF16)
        place = sb("place", [P, 9])
        prod = sb("prod", [P, 9])
        count = sb("count", [P, 9])
        slot_f = sb("slot_f", [P, 2])
        slot_i = sb("slot_i", [P, UNROLL, 2], I32)
        entry = sb("entry", [P, UNROLL, 2, 2], I32)
        tt_n = spread[0:1, 1024:1168].rearrange("p (e i) -> p e i", i=16)
        tt_tiles = spread[0:1, 1168:1177]
        tt_tri = spread[0:1, 1184:1265].rearrange("p (x y) -> p x y", y=9)
        tt_end = spread[0:1, 1280:1289]
        tt_ge = spread[0:1, 0:9 * JMAX].rearrange("p (j e) -> p j e", e=9)
        tt_gt = spread[0:1, 9 * JMAX:18 * JMAX].rearrange("p (j e) -> p j e", e=9)
        tt_e, tt_s, tt_r, tt_r2 = (spread[0:1, at:at + JMAX] for at in (1296, 1344, 1392, 1440))
        tile_row = sb("tile_row", [1, JMAX], I32)
        tile_exp = sb("tile_exp", [1, JMAX], I32)
        places = sb("places", [P, JMAX, 2], I32)
        idx_g = sb("idx_g", [P, 1], I32)
        idx_s = sb("idx_s", [P, 1], I32)
        gate_in = spread[:, 0:512]
        gated = spread[:, 512:1216]
        up_in = spread[:, 1216:1728]
        act = spread[:, 1728:2496]
        actT = spread[:, 2496:3264].rearrange("p (c n) -> p c n", n=P)

        xg = spread[:, 3264:3520]
        xgT = spread[:, 3520:3776].rearrange("p (c n) -> p c n", c=KD)
        y_sb = spread[:, 3776:4032]

        def const(name):
            at, n = CONSTS[name]
            return consts[:, at:at + n]

        tail = experts[:, 8 * SLOT:9 * SLOT]
        w_tok = tail[:, 0:KF * D].rearrange("p (k n) -> p k n", k=KF)
        patch = tail[:, KF * D:KF * D + 2 * FEAT].rearrange("p (s k n) -> p s k n", s=2, k=KF)
        pos = tail[:, KF * D + 2 * FEAT:KF * D + 2 * FEAT + D]
        bias_tok = tail[:, KF * D + 2 * FEAT + D:KF * D + 2 * FEAT + 2 * D]
        by_expert = experts[:, :].rearrange("p (e n) -> p e n", n=SLOT)

        bank = [ctx.enter_context(nc.psum_tensor(f"bank{i}", [P, 512], F32)) for i in range(4)]
        pair45 = ctx.enter_context(nc.psum_tensor("bank45", [P, 2, 512], F32))
        pair67 = ctx.enter_context(nc.psum_tensor("bank67", [P, 2, 512], F32))
        ps_tok, ps_v = bank[0][:, 0:D], bank[0][:, D:2 * D]
        ps_xT, ps_x2T = bank[1][:, 0:D], bank[1][:, D:2 * D]
        ps_qk, ps_swap = bank[2], bank[3]
        ps_sc = pair45[:, :, :]
        ps_pT, ps_proj = pair45[:, 0, 0:D], pair45[:, 1, 0:D]
        ps_o = pair67[:, :, :]
        ps_oT, ps_route, ps_rank = pair67[:, 0, 0:D], pair67[:, 1, 0:9], bank[3][:, 0:32]
        ps_g, ps_u = pair45, pair67
        ps_aT = [bank[0], bank[1]]
        ps_y, ps_gT = bank[2], bank[3]

        consts_in = sem("consts_in")
        small_in = sem2("small_in")
        tokw_in = sem("tokw_in")
        cast_done = sem("cast_done")
        pad_done = sem("pad_done")
        pos_done = sem("pos_done")
        patch_in = [sem("patch_in_even"), sem("patch_in_odd")]
        h_in = [sem(f"h_in_{s}") for s in range(UNROLL)]
        experts_in = sem2("experts_in")
        dummies_in = sem("dummies_in")
        tok_mm = sem("tok_mm")
        h_ready = sem2("h_ready")
        hb_ready = sem2("hb_ready")
        ln_step = sem2("ln_step")
        rstd_ready, rstd2_ready = sem2("rstd_ready"), sem2("rstd2_ready")
        xT_mm, xT_ready = sem2("xT_mm"), sem2("xT_ready")
        qk_mm, qk_ready = sem2("qk_mm"), sem2("qk_ready")
        swap_mm, cos_ready, rot_ready = sem("swap_mm"), sem("cos_ready"), sem("rot_ready")
        rope_done = sem("rope_done")
        qblk_ready = sem2("qblk_ready")
        v_mm, v_ready = sem2("v_mm"), sem2("v_ready")
        sc_mm, sm_step, exp_ready, p_ready = sem2("sc_mm"), sem2("sm_step"), sem2("exp_ready"), sem2("p_ready")
        pT_mm, pblk_ready = sem2("pT_mm"), sem2("pblk_ready")
        o_mm, o_ready = sem2("o_mm"), sem2("o_ready")
        oT_mm, oT_ready = sem2("oT_mm"), sem2("oT_ready")
        proj_mm, h2_ready = sem2("proj_mm"), sem2("h2_ready")
        ln2_step = sem2("ln2_step")
        h2_out = [[sem(f"h2_out_{layer}_{s}") for s in range(UNROLL)] for layer in range(2)]
        xln2_out = [[sem(f"xln2_out_{layer}_{s}") for s in range(2)] for layer in range(2)]
        x2T_mm, x2T_ready = sem2("x2T_mm"), sem2("x2T_ready")
        route_mm, rt_step, egap_ready = sem2("route_mm"), sem2("rt_step"), sem2("egap_ready")
        rank_mm, entry_ready, entry_out = sem2("rank_mm"), sem2("entry_ready"), sem2("entry_out")
        slot_step, wgt_in = sem2("slot_step"), sem2("wgt_in")
        tt_step, tt_sum = sem2("tt_step"), sem2("tt_sum")
        count_zero, act_pad, w_pad = sem("count_zero"), sem("act_pad"), sem("w_pad")
        waited = sem("waited")
        places_in = [[sem(f"places_in_{layer}_{s}") for s in ("0", "1", "2", "rest")] for layer in range(2)]
        idx_g_ready, gather_in = sem2("idx_g_ready"), sem2("gather_in")
        gT_mm, gT_ready = sem2("gT_mm"), sem2("gT_ready")
        g_mm, u_mm = sem2("g_mm"), sem2("u_mm")
        gbias_ready, ubias_ready, silu_ready, act_ready = sem2("gbias_ready"), sem2("ubias_ready"), sem2("silu_ready"), sem2("act_ready")
        aT_mm, aT_ready = sem2("aT_mm"), sem2("aT_ready")
        y_mm, yb_ready, y_ready = sem2("y_mm"), sem2("yb_ready"), sem2("y_ready")
        idx_s_ready, added = sem2("idx_s_ready"), sem2("added")

        N_CONST = 16
        SMALL = 6 * 16
        LN_STEPS = 4
        SM_STEPS = 6
        RT_STEPS = 14
        BLK = HPC
        TT_STEPS = 11
        W_DMAS = (4 * E[0] * 16, 4 * E[1] * 16)
        RESID = [tables["resid"], out]
        NORMED = [tables["normed0"], tables["normed1"]]
        TABLE = [tables["table0"], tables["table1"]]

        def steps(engine, step):
            total = NT + LAG_RANK
            for i in range(UNROLL):
                step(i, i)
            with engine.Fori(1, NT // UNROLL) as group:
                for d in range(UNROLL):
                    step(group * UNROLL + d, d)
            for i in range(NT, total):
                step(i, i % UNROLL)

        def live(i, lag):
            return not isinstance(i, int) or 0 <= i - lag < NT

        def wait_turn(engine, semaphores, i, d, lag):
            n = len(semaphores)
            at = d - lag
            if live(i, lag):
                if isinstance(i, int):
                    engine.wait_ge(semaphores[at % n], 16 * ((i - lag) // n + 1))
                else:
                    engine.wait_ge(semaphores[at % n], (i - d) * (16 // n) + 16 * (at // n + 1))

        def wait(engine, semaphore, value):
            if not isinstance(value, int) or value > 0:
                engine.wait_ge(semaphore, value)

        def apart(engine):
            engine.sem_inc(waited, 1)

        block = ctx.enter_context(nc.Block())

        @block.sync
        def _(sp):
            sp.dma_start(consts[:], a["consts"]).then_inc(consts_in, N_CONST)
            sp.dma_start(w_tok, a["w_tok"]).then_inc(tokw_in, 16)
            sp.dma_start(pos, a["pos"]).then_inc(tokw_in, 16)
            sp.dma_start(bias_tok, a["b_tok"].partition_broadcast(P)).then_inc(tokw_in, 16)

            def small(layer):
                sp.dma_start(w_qkv[:], a[f"w_qkv{layer}"]).then_inc(small_in[layer], 16)
                sp.dma_start(bias_qk[:], a[f"b_qk{layer}"]).then_inc(small_in[layer], 16)
                sp.dma_start(bias_v[:], a[f"b_v{layer}"].partition_broadcast(P)).then_inc(small_in[layer], 16)
                sp.dma_start(bias_proj[:], a[f"b_proj{layer}"].partition_broadcast(P)).then_inc(small_in[layer], 16)
                sp.dma_start(w_proj[:], a[f"w_proj{layer}"]).then_inc(small_in[layer], 16)
                sp.dma_start(w_gate[:, :, 0:E[layer]], a[f"w_gate{layer}"]).then_inc(small_in[layer], 16)
                if layer == 0:
                    sp.dma_start(bias_gate[:], a["b_gate"].partition_broadcast(P)).then_inc(small_in[0], 16)

            def attention(layer):
                def step(i, d):
                    if layer == 0 and live(i, 0):
                        wait(sp, tok_mm, i - 1)
                        sp.dma_start(patch[:, d % 2], a["patches"][bass.ts(i, P), :].rearrange("p (k n) -> p k n", k=KF)).then_inc(patch_in[d % 2], 16)
                        if isinstance(i, int) and i == 1:
                            small(0)
                            for table, n in ((0, E[0]), (1, E[1])):
                                sp.dma_start(TABLE[table], a[f"empty{table}"]).then_inc(dummies_in, 16)
                            for rows in (RESID[0], NORMED[0], NORMED[1], RESID[1]):
                                sp.dma_start(rows[DUMMY:ROWS, :], a["zeros"]).then_inc(dummies_in, 16)
                    if layer == 1 and live(i, 0):
                        wait_turn(sp, h2_out[1], i, d, 4)
                        apart(sp)
                        wait(sp, ln2_step[1], LN_STEPS * (i - 3))
                        sp.dma_start(h[:, d], RESID[0][bass.ts(i, P), :]).then_inc(h_in[d], 16)
                    if live(i, 2):
                        wait(sp, h2_ready[layer], i - 1)
                        sp.dma_start(RESID[layer][bass.ts(i - 2, P), :], h[:, (d - 2) % UNROLL]).then_inc(h2_out[layer][(d - 2) % UNROLL], 16)
                        wait(sp, ln2_step[layer], LN_STEPS * (i - 1))
                        sp.dma_start(NORMED[layer][bass.ts(i - 2, P), :], xln2[:, d % 2]).then_inc(xln2_out[layer][d % 2], 16)
                steps(sp, step)

            def moe(layer):
                sp.wait_ge(tt_step[layer], TT_STEPS)
                sp.wait_ge(entry_out[layer], 32 * NT)
                if layer == 1:
                    sp.wait_ge(idx_s_ready[0], NTILE[0])
                    sp.wait_ge(y_ready[0], NTILE[0])

                def load(j, done):
                    row = sp.value_load(tile_row[0:1, bass.ds(j, 1)], min_val=0, max_val=(E[layer] + 1) * TOK - P)
                    sp.dma_start(places[:, bass.ds(j, 1), :], TABLE[layer][bass.ds(row, P), :].rearrange("p (o n) -> p o n", o=1)).then_inc(done, 16)

                for j in range(3):
                    load(j, places_in[layer][j])
                with sp.Fori(3, NTILE[layer]) as j:
                    load(j, places_in[layer][3])

            attention(0)
            moe(0)
            sp.wait_ge(added[0], 16 * NTILE[0])
            sp.wait_ge(oT_mm[0], NT)
            small(1)
            attention(1)
            moe(1)
            for stored in h2_out[1]:
                sp.wait_ge(stored, 16 * NT // UNROLL)
            sp.wait_ge(dummies_in, 6 * 16)
            sp.wait_ge(added[1], 16 * NTILE[1])

        @block.gpsimd
        def _(pool):
            nc.gpsimd.memset(k_sb[:, :, P:P + PAD], 0.0).then_inc(pad_done, 1)
            nc.gpsimd.memset(v_sb[:, :, D:D + PAD], 0.0).then_inc(pad_done, 1)
            pool.wait_ge(consts_in, N_CONST)
            nc.gpsimd.tensor_copy(upper_bf[:], const("upper")).then_inc(cast_done, 1)
            nc.gpsimd.tensor_copy(ones_bf[:], const("ones")).then_inc(cast_done, 1)
            nc.gpsimd.tensor_copy(tok_id[:], const("tokid")).then_inc(cast_done, 1)
            pool.wait_ge(tokw_in, 48)
            nc.gpsimd.tensor_tensor(pos, pos, bias_tok, ALU.add).then_inc(pos_done, 1)

            def attention(layer):
                def step(i, d):
                    if live(i, 0):
                        wait(pool, ln_step[layer], LN_STEPS * i + 3)
                        nc.gpsimd.tensor_tensor(rstd[:, 0:1], var_eps[:, 0:1], const("nhalf"), ALU.pow).then_inc(rstd_ready[layer], 1)
                        if layer == 0:
                            if isinstance(i, int) and i == 0:
                                pool.wait_ge(small_in[0], SMALL + 16)
                        elif isinstance(i, int) and i == 0:
                            pool.wait_ge(small_in[1], SMALL)
                        wait(pool, ln_step[layer], LN_STEPS * (i + 1))
                        nc.gpsimd.tensor_tensor(h[:, d], h[:, d], bias_proj[:], ALU.add).then_inc(hb_ready[layer], 1)
                        if layer == 1:
                            wait(pool, qk_ready[1], 4 * (i + 1))
                            wait(pool, swap_mm, i + 1)
                            raw = qk_raw[:].rearrange("p c (b n) -> p (c b) n", n=NPATCH)
                            nc.gpsimd.tensor_tensor(raw, raw, const("cos").unsqueeze(1).to_broadcast([P, 4 * IPT, NPATCH]), ALU.mult).then_inc(cos_ready, 1)
                    if live(i, 2):
                        wait(pool, ln2_step[layer], LN_STEPS * (i - 2) + 3)
                        nc.gpsimd.tensor_tensor(rstd[:, 1:2], var_eps[:, 1:2], const("nhalf"), ALU.pow).then_inc(rstd2_ready[layer], 1)
                    if live(i, 4):
                        wait(pool, entry_ready[layer], i - 3)
                        for c in range(2):
                            apart(pool)
                            nc.gpsimd.indirect_dma_start(
                                out=TABLE[layer], out_offset=bass.IndirectOffsetOnAxis(slot_i[:, d, c:c + 1], 0),
                                in_=entry[:, d, c], in_offset=None).then_inc(entry_out[layer], 16)
                        pool.wait_ge(entry_out[layer], 32 * (i - 3))
                steps(pool, step)

            def moe(layer):
                n = NTILE[layer]
                for stored in xln2_out[layer] + h2_out[layer]:
                    pool.wait_ge(stored, 16 * NT // (2 if stored in xln2_out[layer] else UNROLL))

                def gather(j):
                    if isinstance(j, int):
                        pool.wait_ge(places_in[layer][j], 16)
                    else:
                        pool.wait_ge(places_in[layer][3], 16 * (n - 3))
                    wait(pool, gather_in[layer], 16 * j)
                    nc.gpsimd.tensor_copy(idx_g[:], places[:, bass.ds(j, 1), 0]).then_inc(idx_g_ready[layer], 1)
                    wait(pool, gT_mm[layer], j)
                    pool.wait_ge(idx_g_ready[layer], j + 1)
                    apart(pool)
                    nc.gpsimd.indirect_dma_start(out=xg, out_offset=None, in_=NORMED[layer],
                                                 in_offset=bass.IndirectOffsetOnAxis(idx_g[:, 0:1], 0)).then_inc(gather_in[layer], 16)

                def add(j):
                    wait(pool, added[layer], 16 * j)
                    nc.gpsimd.tensor_copy(idx_s[:], places[:, bass.ds(j, 1), 0]).then_inc(idx_s_ready[layer], 1)
                    pool.wait_ge(y_ready[layer], j + 1)
                    pool.wait_ge(idx_s_ready[layer], j + 1)
                    apart(pool)
                    nc.gpsimd.indirect_dma_start(out=RESID[layer], out_offset=bass.IndirectOffsetOnAxis(idx_s[:, 0:1], 0),
                                                 in_=y_sb, in_offset=None, compute_op=ALU.add).then_inc(added[layer], 16)

                gather(0)
                gather(1)
                gather(2)
                add(0)
                with pool.Fori(3, n) as j:
                    gather(j)
                    add(j - 2)
                add(n - 2)
                add(n - 1)

            pool.wait_ge(dummies_in, 6 * 16)
            for layer in range(2):
                if layer == 1:
                    pool.wait_ge(y_mm[0], NTILE[0])
                    nc.gpsimd.memset(by_expert[64:P, :, SLOT - D:SLOT], 0.0).then_inc(w_pad, 1)
                    pool.wait_ge(w_pad, 1)
                attention(layer)
                moe(layer)

        @block.scalar
        def _(act_e):
            def load_experts(layer):
                for e in range(E[layer]):
                    slot = by_expert[:, e]
                    at = 0
                    for name, n in ((("w_up0", 1024), ("w_gate_h0", 1024), ("w_down0", 1024)) if layer == 0 else
                                    (("w_gate_h1", 1408), ("w_up1", 1408))):
                        act_e.dma_start(slot[:, at:at + n], a[name][e]).then_inc(experts_in[layer], 16)
                        at += n
                    if layer == 0:
                        act_e.dma_start(slot[:, at:at + 1280], a["b_exp"][e:e + 1, :].partition_broadcast(P)).then_inc(experts_in[0], 16)
                    else:
                        act_e.dma_start(slot[:, at:at + 1280].rearrange("p (k n) -> p k n", n=D), a["w_down1"][e, 0:640, :].rearrange("(k p) n -> p k n", p=P)).then_inc(experts_in[1], 16)
                        act_e.dma_start(slot[0:64, at + 1280:at + 1536], a["w_down1"][e, 640:704, :]).then_inc(experts_in[1], 16)

            def attention(layer):
                def step(i, d):
                    if live(i, 0):
                        wait(act_e, xT_mm[layer], i + 1)
                        wait(act_e, v_mm[layer], i)
                        nc.scalar.activation(xlnT[:].rearrange("p c n -> p (c n)"), ps_xT, ACT.Copy).then_inc(xT_ready[layer], 1)
                    if live(i, 1):
                        wait(act_e, sm_step[layer], SM_STEPS * (i - 1) + 4)
                        nc.scalar.activation(s_sb[:], s_sb[:], ACT.Exp).then_inc(exp_ready[layer], 1)
                    if live(i, 2):
                        wait(act_e, o_mm[layer], i - 1)
                        wait(act_e, oT_mm[layer], i - 2)
                        nc.scalar.activation(o_sb[:].rearrange("p (s g n) -> p s g n", s=2, n=HD),
                                             ps_o.rearrange("p s (g w) -> p s g w", w=WIN)[:, :, :, 0:HD], ACT.Copy).then_inc(o_ready[layer], 1)
                    if live(i, 0):
                        wait(act_e, qk_mm[layer], i + 1)
                        if layer == 0:
                            wait(act_e, qblk_ready[0], BLK * i)
                            wait(act_e, sc_mm[0], 2 * i)
                        else:
                            wait(act_e, rope_done, 2 * i)
                        if isinstance(i, int) and i == 0:
                            act_e.wait_ge(small_in[layer], SMALL + 16 * (1 - layer))
                            act_e.wait_ge(pad_done, 2)
                        for c in range(4):
                            to = qk_raw[:, c] if layer else (q_sb[:, c] if c < 2 else k_sb[:, c - 2, 0:P])
                            nc.scalar.activation(to, ps_qk[:, c * P:(c + 1) * P], ACT.Identity, bias=bias_qk[:, c:c + 1]).then_inc(qk_ready[layer], 1)
                    if live(i, 2):
                        wait(act_e, oT_mm[layer], i - 1)
                        wait(act_e, proj_mm[layer], i - 2)
                        nc.scalar.activation(oT[:].rearrange("p c n -> p (c n)"), ps_oT, ACT.Copy).then_inc(oT_ready[layer], 1)
                    if live(i, 1):
                        wait(act_e, pT_mm[layer], i)
                        wait(act_e, o_mm[layer], i - 1)
                        for b in range(IPT):
                            nc.scalar.activation(pblk[:, :, b], ps_pT.rearrange("p (g n) -> p g n", n=16), ACT.Copy, scale=const("block")[:, b:b + 1]).then_inc(pblk_ready[layer], 1)
                    if live(i, 3):
                        wait(act_e, x2T_mm[layer], i - 2)
                        wait(act_e, route_mm[layer], i - 3)
                        nc.scalar.activation(xln2T[:].rearrange("p c n -> p (c n)"), ps_x2T, ACT.Copy).then_inc(x2T_ready[layer], 1)
                        wait(act_e, rt_step[layer], RT_STEPS * (i - 3) + 4)
                        nc.scalar.activation(egap[:], gap[:], ACT.Exp).then_inc(egap_ready[layer], 1)
                steps(act_e, step)

            def moe(layer):
                n = NTILE[layer]
                hid = HID[layer]
                gv = gated[:, 0:hid] if layer == 0 else gated[:, 0:hid].rearrange("p (s n) -> p s n", s=2)

                def gate(j):
                    wait(act_e, act_ready[layer], j)
                    if layer == 0:
                        act_e.wait_ge(gbias_ready[0], j + 1)
                        nc.scalar.activation(gv, gate_in, ACT.Silu).then_inc(silu_ready[0], 1)
                    else:
                        act_e.wait_ge(g_mm[1], j + 1)
                        nc.scalar.activation(gv, ps_g[:, :, 0:hid // 2], ACT.Silu).then_inc(silu_ready[1], 1)

                def turned(j):
                    act_e.wait_ge(aT_mm[layer], j + 1)
                    half = actT.rearrange("p c n -> p (c n)")
                    nc.scalar.activation(half[:, 0:512], ps_aT[0][:, 0:512], ACT.Copy).then_inc(aT_ready[layer], 1)
                    if layer == 1:
                        nc.scalar.activation(half[:, 512:768], ps_aT[1][:, 0:256], ACT.Copy).then_inc(aT_ready[1], 1)

                gate(0)
                with act_e.Fori(1, n) as j:
                    gate(j)
                    turned(j - 1)
                turned(n - 1)

            load_experts(0)
            attention(0)
            moe(0)
            act_e.wait_ge(y_mm[0], NTILE[0])
            act_e.wait_ge(yb_ready[0], NTILE[0])
            load_experts(1)
            attention(1)
            moe(1)

        @block.vector
        def _(dve):
            def layer_norm(x, to, slot, semaphore, inverse, i):
                s = LN_STEPS * i
                nc.vector.bn_stats(stats[:, slot], x).then_inc(semaphore, 1)
                dve.wait_ge(semaphore, s + 1)
                apart(dve)
                nc.vector.bn_aggr(moments[:, slot], stats[:, slot]).then_inc(semaphore, 1)
                dve.wait_ge(semaphore, s + 2)
                nc.vector.tensor_scalar(var_eps[:, slot:slot + 1], moments[:, slot, 1:2], EPS, None, ALU.add).then_inc(semaphore, 1)
                dve.wait_ge(inverse, i + 1)
                nc.vector.tensor_scalar(to, x, moments[:, slot, 0:1], rstd[:, slot:slot + 1], ALU.subtract, ALU.mult).then_inc(semaphore, 1)

            def softmax(layer, t):
                s = SM_STEPS * t
                step_sem = sm_step[layer]
                mask = const(f"mask{layer}").rearrange("p (c k) -> p c k", c=2)
                for c in range(2):
                    dve.wait_ge(sc_mm[layer], 2 * t + c + 1)
                    nc.vector.scalar_tensor_tensor(
                        s_sb[:, c * IPT:(c + 1) * IPT], ps_sc[:, c].rearrange("p (b w) -> p b w", w=WIN)[:, :, 0:16], float(HD) ** -0.5,
                        mask[:, c:c + 1, :].to_broadcast([P, IPT, 16]), ALU.mult, ALU.add).then_inc(step_sem, 1)
                dve.wait_ge(step_sem, s + 2)
                nc.vector.tensor_reduce(s_max[:], s_sb[:], AX.X, ALU.max).then_inc(step_sem, 1)
                dve.wait_ge(step_sem, s + 3)
                nc.vector.tensor_tensor(s_sb[:], s_sb[:], s_max[:].unsqueeze(2).to_broadcast([P, 16, 16]), ALU.subtract).then_inc(step_sem, 1)
                dve.wait_ge(exp_ready[layer], t + 1)
                nc.vector.tensor_reduce(s_sum[:], s_sb[:], AX.X, ALU.add).then_inc(step_sem, 1)
                dve.wait_ge(step_sem, s + 5)
                nc.vector.reciprocal(s_inv[:], s_sum[:]).then_inc(step_sem, 1)
                dve.wait_ge(step_sem, s + 6)
                wait(dve, pT_mm[layer], t)
                nc.vector.tensor_tensor(p_sb[:], s_sb[:], s_inv[:].unsqueeze(2).to_broadcast([P, 16, 16]), ALU.mult).then_inc(p_ready[layer], 1)

            def route(layer, t):
                e = E[layer]
                s = RT_STEPS * t
                st = rt_step[layer]
                dve.wait_ge(route_mm[layer], t + 1)
                if layer == 0:
                    nc.vector.tensor_tensor(logits[:, 0:e], ps_route[:, 0:e], bias_gate[:], ALU.add).then_inc(st, 1)
                else:
                    nc.vector.tensor_copy(logits[:, 0:e], ps_route[:, 0:e]).then_inc(st, 1)
                dve.wait_ge(st, s + 1)
                apart(dve)
                nc.vector.max(top[:], logits[:, 0:e]).then_inc(st, 1)
                dve.wait_ge(st, s + 2)
                apart(dve)
                nc.vector.max_index(top_i[:], top[:], logits[:, 0:e]).then_inc(st, 1)
                nc.vector.tensor_tensor(gap[:], top[:, 1:2], top[:, 0:1], ALU.subtract).then_inc(st, 1)
                dve.wait_ge(st, s + 4)
                nc.vector.tensor_copy(top_f[:], top_i[:, 0:2]).then_inc(st, 1)
                dve.wait_ge(st, s + 5)
                for c in range(2):
                    nc.vector.tensor_scalar(pick[:, c, 0:e], const("eidx")[:, 0:e], top_f[:, c:c + 1], None, ALU.is_equal).then_inc(st, 1)
                dve.wait_ge(st, s + 7)
                nc.vector.tensor_tensor(both_bf[:, 0:e], pick[:, 0, 0:e], pick[:, 1, 0:e], ALU.add).then_inc(st, 1)
                dve.wait_ge(egap_ready[layer], t + 1)
                nc.vector.tensor_scalar(wgt[:, 1:2], egap[:], 1.0, None, ALU.add).then_inc(st, 1)
                dve.wait_ge(st, s + 9)
                nc.vector.reciprocal(wgt[:, 0:1], wgt[:, 1:2]).then_inc(st, 1)
                dve.wait_ge(st, s + 10)
                nc.vector.tensor_tensor(wgt[:, 1:2], wgt[:, 0:1], egap[:], ALU.mult).then_inc(st, 1)

            def entries(layer, t, slot):
                e = E[layer]
                s = RT_STEPS * t
                st = rt_step[layer]
                dve.wait_ge(rank_mm[layer], t + 1)
                nc.vector.tensor_tensor(place[:, 0:e], ps_rank[:, 0:e], count[:, 0:e], ALU.add).then_inc(st, 1)
                dve.wait_ge(st, s + 12)
                nc.vector.tensor_tensor(count[:, 0:e], count[:, 0:e], ps_rank[:, 16:16 + e], ALU.add).then_inc(st, 1)
                nc.vector.tensor_tensor(place[:, 0:e], place[:, 0:e], const("eoff")[:, 0:e], ALU.add).then_inc(st, 1)
                dve.wait_ge(st, s + 14)

                for c in range(2):
                    nc.vector.tensor_tensor_reduce(prod[:, 0:e], pick[:, c, 0:e], place[:, 0:e], 1.0, 0.0, ALU.mult, ALU.add,
                                                   slot_f[:, c:c + 1]).then_inc(slot_step[layer], 1)
                    dve.wait_ge(slot_step[layer], 3 * t + c + 1)
                nc.vector.tensor_copy(slot_i[:, slot], slot_f[:]).then_inc(slot_step[layer], 1)
                dve.wait_ge(slot_step[layer], 3 * t + 3)
                nc.vector.tensor_copy(entry[:, slot, :, 1].bitcast(F32), wgt[:]).then_inc(wgt_in[layer], 1)
                dve.wait_ge(wgt_in[layer], t + 1)
                nc.vector.tensor_copy(entry[:, slot, :, 0], tok_id[:, bass.ds(t, 1)].to_broadcast([P, 2])).then_inc(entry_ready[layer], 1)

            def attention(layer):
                def step(i, d):
                    if live(i, 0):
                        if layer == 0:
                            wait(dve, tok_mm, i + 1)
                            wait_turn(dve, h2_out[0], i, d, 4)
                            wait(dve, ln2_step[0], LN_STEPS * (i - 3))
                            nc.vector.tensor_tensor(h[:, d], ps_tok, pos, ALU.add).then_inc(h_ready[0], 1)
                            dve.wait_ge(h_ready[0], i + 1)
                        else:
                            if isinstance(i, int):
                                dve.wait_ge(h_in[d], 16 * (i // UNROLL + 1))
                            else:
                                dve.wait_ge(h_in[d], (i - d) * (16 // UNROLL) + 16)
                        wait(dve, xT_mm[layer], i)
                        layer_norm(h[:, d], xln[:], 0, ln_step[layer], rstd_ready[layer], i)
                    if live(i, 4):
                        entries(layer, i - 4, d)
                    if live(i, 1):
                        softmax(layer, i - 1)
                    if live(i, 0) and layer == 0:
                        wait(dve, qk_ready[0], 4 * i + 2)
                        wait(dve, sc_mm[layer], 2 * i)
                        for g in range(HPC):
                            nc.vector.tensor_scalar(qblk[:, :, g], q_sb[:].rearrange("p c (b n) -> p (c b) n", n=16), const("block")[:, g:g + 1], None, ALU.mult).then_inc(qblk_ready[0], 1)
                    if live(i, 0):
                        wait(dve, v_mm[layer], i + 1)
                        nc.vector.tensor_tensor(v_sb[:, d % 2, 0:D], ps_v, bias_v[:], ALU.add).then_inc(v_ready[layer], 1)
                    if live(i, 0) and layer == 1:
                        wait(dve, swap_mm, i + 1)
                        rotv = rot[:].rearrange("p c (b n) -> p (c b) n", n=NPATCH)
                        nc.vector.tensor_tensor(rotv, ps_swap[:].rearrange("p (b n) -> p b n", n=NPATCH),
                                                const("sin").unsqueeze(1).to_broadcast([P, 4 * IPT, NPATCH]), ALU.mult).then_inc(rot_ready, 1)
                        wait(dve, rot_ready, i + 1)
                        wait(dve, cos_ready, i + 1)
                        wait(dve, sc_mm[1], 2 * i)
                        nc.vector.tensor_tensor(q_sb[:], rot[:, 0:2], qk_raw[:, 0:2], ALU.add).then_inc(rope_done, 1)
                        nc.vector.tensor_tensor(k_sb[:, :, 0:P], rot[:, 2:4], qk_raw[:, 2:4], ALU.add).then_inc(rope_done, 1)
                        wait(dve, rope_done, 2 * i + 2)
                        wait(dve, sc_mm[layer], 2 * i)
                        for g in range(HPC):
                            nc.vector.tensor_scalar(qblk[:, :, g], q_sb[:].rearrange("p c (b n) -> p (c b) n", n=16), const("block")[:, g:g + 1], None, ALU.mult).then_inc(qblk_ready[1], 1)
                    if live(i, 2):
                        wait(dve, proj_mm[layer], i - 1)
                        wait(dve, hb_ready[layer], i - 1)
                        hh = h[:, (d - 2) % UNROLL]
                        nc.vector.tensor_tensor(hh, ps_proj, hh, ALU.add).then_inc(h2_ready[layer], 1)
                        wait(dve, h2_ready[layer], i - 1)
                        wait_turn(dve, xln2_out[layer], i, d, 4)
                        wait(dve, x2T_mm[layer], i - 3)
                        layer_norm(hh, xln2[:, d % 2], 1, ln2_step[layer], rstd2_ready[layer], i - 2)
                    if live(i, 3):
                        route(layer, i - 3)
                steps(dve, step)

            def tile_table(layer):
                e, n, st = E[layer], NTILE[layer], tt_step[layer]
                dve.wait_ge(slot_step[layer], 3 * NT)
                cnt = count[0:1, 0:e]
                row = lambda name, m: const(name)[0:1, 0:m]
                nc.vector.tensor_tensor(tt_n[:, 0:e], cnt.unsqueeze(2).to_broadcast([1, e, 16]), row("steps", 16).unsqueeze(1).to_broadcast([1, e, 16]), ALU.is_gt).then_inc(st, 1)
                dve.wait_ge(st, 1)
                nc.vector.tensor_reduce(tt_tiles[:, 0:e], tt_n[:, 0:e], AX.X, ALU.add).then_inc(st, 1)
                dve.wait_ge(st, 2)
                tri = row("tri", 81).rearrange("p (x y) -> p x y", y=9)[:, 0:e, 0:e]
                nc.vector.tensor_tensor(tt_tri[:, 0:e, 0:e], tt_tiles[:, 0:e].unsqueeze(1).to_broadcast([1, e, e]), tri, ALU.mult).then_inc(st, 1)
                dve.wait_ge(st, 3)
                nc.vector.tensor_reduce(tt_end[:, 0:e], tt_tri[:, 0:e, 0:e], AX.X, ALU.add).then_inc(st, 1)
                dve.wait_ge(st, 4)
                nc.vector.tensor_tensor(tt_ge[:, 0:n, 0:e], row("tile", n).unsqueeze(2).to_broadcast([1, n, e]), tt_end[:, 0:e].unsqueeze(1).to_broadcast([1, n, e]), ALU.is_ge).then_inc(st, 1)
                dve.wait_ge(st, 5)
                nc.vector.tensor_reduce(tt_e[:, 0:n], tt_ge[:, 0:n, 0:e], AX.X, ALU.add).then_inc(st, 1)
                nc.vector.tensor_tensor(tt_gt[:, 0:n, 0:e], tt_ge[:, 0:n, 0:e], tt_tiles[:, 0:e].unsqueeze(1).to_broadcast([1, n, e]), ALU.mult).then_inc(st, 1)
                dve.wait_ge(st, 7)
                nc.vector.tensor_reduce(tt_s[:, 0:n], tt_gt[:, 0:n, 0:e], AX.X, ALU.add).then_inc(st, 1)
                nc.vector.tensor_scalar(tile_exp[:, 0:n], tt_e[:, 0:n], float(e - 1), None, ALU.min).then_inc(st, 1)
                dve.wait_ge(st, 8)
                nc.vector.tensor_tensor(tt_r[:, 0:n], row("tile", n), tt_s[:, 0:n], ALU.subtract).then_inc(st, 1)
                dve.wait_ge(st, 10)
                nc.vector.scalar_tensor_tensor(tt_r2[:, 0:n], tt_e[:, 0:n], float(TOK // P), tt_r[:, 0:n], ALU.mult, ALU.add).then_inc(tt_sum[layer], 1)
                dve.wait_ge(tt_sum[layer], 1)
                nc.vector.tensor_scalar(tile_row[:, 0:n], tt_r2[:, 0:n], float(P), None, ALU.mult).then_inc(st, 1)

            def moe(layer):
                n, hid = NTILE[layer], HID[layer]
                half = hid // 2
                if layer == 1:
                    dve.wait_ge(tt_step[1], TT_STEPS)
                    nc.vector.memset(act[:, hid:HPAD[1]], 0.0).then_inc(act_pad, 1)
                else:
                    dve.wait_ge(experts_in[0], W_DMAS[0])

                def expert_of(j):
                    return dve.value_load(tile_exp[0:1, bass.ds(j, 1)], min_val=0, max_val=E[layer] - 1)

                def bias(e, at, m):
                    return experts[:, bass.ds(e * SLOT + 3072 + at, m)]

                def hidden(j, e):
                    if layer == 0:
                        dve.wait_ge(g_mm[0], j + 1)
                        wait(dve, silu_ready[0], j)
                        nc.vector.tensor_tensor(gate_in, ps_g[:, 0], bias(e, 512, 512), ALU.add).then_inc(gbias_ready[0], 1)
                        dve.wait_ge(u_mm[0], j + 1)
                        nc.vector.tensor_tensor(up_in, ps_u[:, 0], bias(e, 0, 512), ALU.add).then_inc(ubias_ready[0], 1)
                        dve.wait_ge(ubias_ready[0], j + 1)
                        dve.wait_ge(silu_ready[0], j + 1)
                        nc.vector.tensor_tensor(act[:, 0:hid], up_in, gated[:, 0:hid], ALU.mult).then_inc(act_ready[0], 1)
                    else:
                        dve.wait_ge(u_mm[1], j + 1)
                        dve.wait_ge(silu_ready[1], j + 1)
                        nc.vector.tensor_tensor(act[:, 0:hid].rearrange("p (s n) -> p s n", s=2), ps_u[:, :, 0:half],
                                                gated[:, 0:hid].rearrange("p (s n) -> p s n", s=2), ALU.mult).then_inc(act_ready[1], 1)

                def turned(j):
                    dve.wait_ge(gT_mm[layer], j + 1)
                    nc.vector.tensor_copy(xgT.rearrange("p c n -> p (c n)"), ps_gT[:, 0:D]).then_inc(gT_ready[layer], 1)

                def weighted(j, e):
                    dve.wait_ge(y_mm[layer], j + 1)
                    wait(dve, added[layer], 16 * j)
                    w = places[:, bass.ds(j, 1), 1].bitcast(F32)
                    if layer == 0:
                        nc.vector.tensor_tensor(y_sb, ps_y[:, 0:D], bias(e, 1024, D), ALU.add).then_inc(yb_ready[0], 1)
                        dve.wait_ge(yb_ready[0], j + 1)
                        nc.vector.tensor_scalar(y_sb, y_sb, w, None, ALU.mult).then_inc(y_ready[0], 1)
                    else:
                        nc.vector.tensor_scalar(y_sb, ps_y[:, 0:D], w, None, ALU.mult).then_inc(y_ready[1], 1)

                turned(0)
                hidden(0, expert_of(0))
                turned(1)
                with dve.Fori(1, n - 1) as j:
                    hidden(j, expert_of(j))
                    turned(j + 1)
                    weighted(j - 1, expert_of(j - 1))
                hidden(n - 1, expert_of(n - 1))
                weighted(n - 2, expert_of(n - 2))
                weighted(n - 1, expert_of(n - 1))

            dve.wait_ge(consts_in, N_CONST)
            dve.wait_ge(cast_done, 3)
            dve.wait_ge(pos_done, 1)
            dve.wait_ge(small_in[0], SMALL + 16)
            for layer in range(2):
                if layer == 1:
                    dve.wait_ge(small_in[1], SMALL)
                nc.vector.memset(count[:], 0.0).then_inc(count_zero, 1)
                dve.wait_ge(count_zero, layer + 1)
                attention(layer)
                tile_table(layer)
                moe(layer)

        @block.tensor
        def _(pe):
            ident = const("ident")

            def attention(layer):
                def step(i, d):
                    if layer == 0 and live(i, 0):
                        if isinstance(i, int):
                            pe.wait_ge(patch_in[d % 2], 16 * (i // 2 + 1))
                        else:
                            pe.wait_ge(patch_in[d % 2], (i - d) * 8 + 16 * (d // 2 + 1))
                        wait(pe, v_ready[0], i)
                        for k in range(KF):
                            mm = nc.tensor.matmul(ps_tok, patch[:, d % 2, k], w_tok[:, k], start=k == 0, stop=k == KF - 1)
                        mm.then_inc(tok_mm, 1)
                    if live(i, 4):
                        e = E[layer]
                        wait(pe, rt_step[layer], RT_STEPS * (i - 4) + 8)
                        if layer == 1:
                            wait(pe, rot_ready, min(i, NT) if isinstance(i, int) else i)
                        nc.tensor.matmul(ps_rank[:, 0:e], upper_bf[:], both_bf[:, 0:e], start=True, stop=True)
                        mm = nc.tensor.matmul(ps_rank[:, 16:16 + e], ones_bf[:], both_bf[:, 0:e], start=True, stop=True)
                        mm.then_inc(rank_mm[layer], 1)
                    if live(i, 1):
                        wait(pe, qblk_ready[layer], BLK * i)
                        wait(pe, qk_ready[layer], 4 * i)
                        if layer == 1:
                            wait(pe, rope_done, 2 * i)
                        wait(pe, pblk_ready[layer], BLK * (i - 1))
                        wait(pe, h2_ready[layer], i - 2)
                        for c in range(KD):
                            for b in range(IPT):
                                mm = nc.tensor.matmul(ps_sc[:, c, b * WIN:(b + 1) * WIN], qblk[:, c * IPT + b].rearrange("p g n -> p (g n)"),
                                                      k_sb[:, c, b * 16:b * 16 + WIN], start=True, stop=True)
                            mm.then_inc(sc_mm[layer], 1)
                    if live(i, 0):
                        wait(pe, ln_step[layer], LN_STEPS * (i + 1))
                        wait(pe, x2T_ready[layer], i - 3)
                        for c in range(KD):
                            mm = nc.tensor.transpose(ps_xT[:, c * P:(c + 1) * P], xln[:, c * P:(c + 1) * P], ident)
                        mm.then_inc(xT_mm[layer], 1)
                    if live(i, 2):
                        wait(pe, pblk_ready[layer], BLK * (i - 1))
                        wait(pe, v_ready[layer], i - 1)
                        wait(pe, oT_ready[layer], i - 2)
                        wait(pe, rt_step[layer], RT_STEPS * (i - 4) + 1)
                        for g in range(NH):
                            mm = nc.tensor.matmul(ps_o[:, g // 8, (g % 8) * WIN:(g % 8 + 1) * WIN],
                                                  pblk[:, g].rearrange("p b n -> p (b n)"),
                                                  v_sb[:, d % 2, g * HD:g * HD + WIN], start=True, stop=True)
                        mm.then_inc(o_mm[layer], 1)
                    if live(i, 0):
                        wait(pe, xT_ready[layer], i + 1)
                        wait(pe, qk_ready[layer], 4 * i)
                        for c in range(4):
                            for k in range(KD):
                                mm = nc.tensor.matmul(ps_qk[:, c * P:(c + 1) * P], w_qkv[:, k, c * P:(c + 1) * P], xlnT[:, k],
                                                      start=k == 0, stop=k == KD - 1)
                        mm.then_inc(qk_mm[layer], 1)
                        for k in range(KD):
                            mm = nc.tensor.matmul(ps_v, xlnT[:, k], w_qkv[:, k, 2 * D:3 * D], start=k == 0, stop=k == KD - 1)
                        mm.then_inc(v_mm[layer], 1)
                    if live(i, 2):
                        wait(pe, o_ready[layer], i - 1)
                        for c in range(KD):
                            mm = nc.tensor.transpose(ps_oT[:, c * P:(c + 1) * P], o_sb[:, c * P:(c + 1) * P], ident)
                        mm.then_inc(oT_mm[layer], 1)
                    if layer == 1 and live(i, 0):
                        wait(pe, qk_ready[1], 4 * (i + 1))
                        wait(pe, rot_ready, i)
                        wait(pe, rt_step[1], RT_STEPS * (i - 4) + 13)
                        mm = nc.tensor.matmul(ps_swap[:], const("swap"), qk_raw[:].rearrange("p c n -> p (c n)"), start=True, stop=True)
                        mm.then_inc(swap_mm, 1)
                    if live(i, 1):
                        wait(pe, p_ready[layer], i)
                        for c in range(2):
                            mm = nc.tensor.transpose(ps_pT[:, c * P:(c + 1) * P],
                                                     p_sb[:, c * IPT:(c + 1) * IPT].rearrange("p b k -> p (b k)"), ident)
                        mm.then_inc(pT_mm[layer], 1)
                    if live(i, 2):
                        wait(pe, oT_ready[layer], i - 1)
                        for k in range(KD):
                            mm = nc.tensor.matmul(ps_proj, oT[:, k], w_proj[:, k], start=k == 0, stop=k == KD - 1)
                        mm.then_inc(proj_mm[layer], 1)
                    if live(i, 3):
                        wait(pe, ln2_step[layer], LN_STEPS * (i - 2))
                        for c in range(KD):
                            mm = nc.tensor.transpose(ps_x2T[:, c * P:(c + 1) * P], xln2[:, (d - 3) % 2, c * P:(c + 1) * P], ident)
                        mm.then_inc(x2T_mm[layer], 1)
                        wait(pe, x2T_ready[layer], i - 2)
                        e = E[layer]
                        for k in range(KD):
                            mm = nc.tensor.matmul(ps_route[:, 0:e], xln2T[:, k], w_gate[:, k, 0:e], start=k == 0, stop=k == KD - 1)
                        mm.then_inc(route_mm[layer], 1)
                steps(pe, step)

            def moe(layer):
                n, hid = NTILE[layer], HID[layer]
                chunks = HPAD[layer] // P
                parts = 1 if layer == 0 else 2
                width = hid // parts
                at_g, at_u, at_d = (KD * hid, 0, 2 * KD * hid) if layer == 0 else (0, KD * hid, 2 * KD * hid)

                def expert_of(j):
                    return pe.value_load(tile_exp[0:1, bass.ds(j, 1)], min_val=0, max_val=E[layer] - 1)

                def turn_in(j):
                    pe.wait_ge(gather_in[layer], 16 * j + 16)
                    wait(pe, gT_ready[layer], j)
                    for c in range(KD):
                        mm = nc.tensor.transpose(ps_gT[:, c * P:(c + 1) * P], xg[:, c * P:(c + 1) * P], ident)
                    mm.then_inc(gT_mm[layer], 1)

                def into(ps, at, e, done):
                    for s in range(parts):
                        for k in range(KD):
                            mm = nc.tensor.matmul(ps[:, s, 0:width], xgT[:, k],
                                                  experts[:, bass.ds(e * SLOT + at + k * hid + s * width, width)],
                                                  start=k == 0, stop=k == KD - 1)
                    mm.then_inc(done, 1)

                def gate(j, e):
                    pe.wait_ge(gT_ready[layer], j + 1)
                    wait(pe, gbias_ready[0] if layer == 0 else silu_ready[1], j)
                    into(ps_g, at_g, e, g_mm[layer])

                def up(j, e):
                    wait(pe, act_ready[layer], j)
                    into(ps_u, at_u, e, u_mm[layer])

                def turn_act(j):
                    pe.wait_ge(act_ready[layer], j + 1)
                    wait(pe, aT_ready[layer], parts * j)
                    for c in range(chunks):
                        mm = nc.tensor.transpose(ps_aT[c // 4][:, (c % 4) * P:(c % 4 + 1) * P], act[:, c * P:(c + 1) * P], ident)
                    mm.then_inc(aT_mm[layer], 1)

                def down(j, e):
                    pe.wait_ge(aT_ready[layer], parts * (j + 1))
                    wait(pe, yb_ready[0] if layer == 0 else y_ready[1], j)
                    for k in range(chunks):
                        mm = nc.tensor.matmul(ps_y[:, 0:D], actT[:, k], experts[:, bass.ds(e * SLOT + at_d + k * D, D)],
                                              start=k == 0, stop=k == chunks - 1)
                    mm.then_inc(y_mm[layer], 1)

                pe.wait_ge(experts_in[layer], W_DMAS[layer])
                pe.wait_ge(tt_step[layer], TT_STEPS)
                if layer == 1:
                    pe.wait_ge(act_pad, 1)
                    pe.wait_ge(w_pad, 1)
                turn_in(0)
                first = expert_of(0)
                gate(0, first)
                up(0, first)
                turn_in(1)
                with pe.Fori(1, n - 1) as j:
                    e = expert_of(j)
                    gate(j, e)
                    turn_act(j - 1)
                    up(j, e)
                    turn_in(j + 1)
                    down(j - 1, expert_of(j - 1))
                last = expert_of(n - 1)
                gate(n - 1, last)
                turn_act(n - 2)
                up(n - 1, last)
                down(n - 2, expert_of(n - 2))
                turn_act(n - 1)
                down(n - 1, last)

            pe.wait_ge(consts_in, N_CONST)
            pe.wait_ge(tokw_in, 48)
            pe.wait_ge(cast_done, 3)
            pe.wait_ge(pad_done, 2)
            pe.wait_ge(small_in[0], SMALL + 16)
            for layer in range(2):
                if layer == 1:
                    pe.wait_ge(small_in[1], SMALL)
                attention(layer)
                moe(layer)


def _constants(np):
    p = np.arange(P)
    c = np.zeros((P, NCONST), np.float32)

    def put(name, v):
        at, n = CONSTS[name]
        c[:, at:at + n] = np.asarray(v, np.float32).reshape(-1, n)

    put("ident", np.eye(P))
    put("swap", np.eye(P)[p ^ 1])
    put("upper", p[:, None] < p[None, :])
    put("ones", np.ones((P, P)))
    pos = np.arange(NPATCH)
    freq = (np.float32(10000.0) ** (-2.0 * np.arange(HD // 2, dtype=np.float32) / HD)).astype(np.float32)
    angle = pos.astype(np.float32)[None, :] * freq[(p % HD) // 2][:, None]
    put("cos", np.cos(angle))
    put("sin", np.sin(angle) * np.where(p % 2 == 0, -1.0, 1.0)[:, None])
    q = (p % 16)[:, None, None]
    head = np.arange(2)[None, :, None] * HPC + (p // 16)[:, None, None]
    k = pos[None, None, :]
    hidden = k > q
    put("mask0", np.where(hidden, -1e30, (k - q) * 0.5 ** (head + 1.0)).reshape(P, 32))
    put("mask1", np.where(hidden + 0 * head, -1e30, 0.0).reshape(P, 32))
    put("block", (p // 16)[:, None] == np.arange(8)[None, :])
    put("tokid", p[:, None] + P * np.arange(NT)[None, :])
    put("eoff", np.arange(9) * TOK)
    put("eidx", np.arange(9))
    put("steps", np.arange(16) * P)
    put("tri", np.arange(9)[:, None] >= np.arange(9)[None, :])
    put("tile", np.arange(JMAX))
    put("nhalf", -0.5)
    return c


def kernel(**inputs):
    import numpy as np
    import concourse.bacc as bacc
    from concourse.bass_utils import run_bass_kernel_spmd as run

    x = {name: np.asarray(v) for name, v in inputs.items()}

    def rows(w):
        return w.reshape(-1, P, w.shape[-1]).transpose(1, 0, 2)

    def experts(w):
        return w.reshape(w.shape[0], -1, P, w.shape[-1]).transpose(0, 2, 1, 3).reshape(w.shape[0], P, -1)

    patches = x["x"].reshape(IMGS, 3, 4, 16, 4, 16).transpose(1, 3, 5, 0, 2, 4)
    patches = patches.reshape(KF, P, NT, P).transpose(2, 1, 0, 3).reshape(NT * P, KF * P)
    a = {
        "consts": _constants(np),
        "zeros": np.zeros((P, D), np.float32),
        "patches": patches,
        "w_tok": rows(x["L0_tok_W"].T),
        "b_tok": x["L0_tok_b"],
        "pos": np.tile(x["L0_tok_pos_emb"], (IPT, 1)),
        "w_gate0": rows(x["L0_ffn_gate_w"].T),
        "b_gate": x["L0_ffn_gate_b"],
        "w_gate1": rows(x["L1_ffn_Wr"]),
        "w_up0": experts(x["L0_ffn_w0"].transpose(0, 2, 1)),
        "w_gate_h0": experts(x["L0_ffn_w1"].transpose(0, 2, 1)),
        "w_down0": experts(x["L0_ffn_w2"].transpose(0, 2, 1)),
        "b_exp": np.concatenate([x["L0_ffn_b0"], x["L0_ffn_b1"], x["L0_ffn_b2"]], axis=1),
        "w_gate_h1": experts(x["L1_ffn_Wg"]),
        "w_up1": experts(x["L1_ffn_Wu"]),
        "w_down1": x["L1_ffn_Wd"],
    }
    for layer, w, b in ((0, "L0_attn_W_attn", "L0_attn_b_attn"), (1, "L1_attn_W_qkv", "L1_attn_b_qkv")):
        a[f"w_qkv{layer}"] = rows(x[w])
        a[f"b_qk{layer}"] = x[b][:2 * D].reshape(4, P).T
        a[f"b_v{layer}"] = x[b][2 * D:]
        a[f"w_proj{layer}"] = rows(x[f"L{layer}_attn_W_proj"])
        a[f"b_proj{layer}"] = x[f"L{layer}_attn_b_proj"]
    for layer in range(2):
        empty = np.zeros(((E[layer] + 1) * TOK, 2), np.int32)
        empty[:, 0] = DUMMY + np.arange(len(empty)) % P
        a[f"empty{layer}"] = empty

    nc = bacc.Bacc("TRN2", target_bir_lowering=False, num_devices=1)
    arrays, aps = {}, {}
    for name, v in a.items():
        v = np.ascontiguousarray(v)
        arrays[f"in_{name}"] = v
        aps[name] = nc.dram_tensor(f"in_{name}", v.shape, mybir.dt.from_np(v.dtype), kind="ExternalInput").ap()
    tables = {
        "resid": nc.dram_tensor("resid", (ROWS, D), F32, kind="Internal").ap(),
        "normed0": nc.dram_tensor("normed0", (ROWS, D), F32, kind="Internal").ap(),
        "normed1": nc.dram_tensor("normed1", (ROWS, D), F32, kind="Internal").ap(),
        "table0": nc.dram_tensor("table0", ((E[0] + 1) * TOK, 2), I32, kind="Internal").ap(),
        "table1": nc.dram_tensor("table1", ((E[1] + 1) * TOK, 2), I32, kind="Internal").ap(),
    }
    out = nc.dram_tensor("out_0", (ROWS, D), F32, kind="ExternalOutput").ap()
    tower(nc, aps, tables, out)
    r = run(nc, [arrays], core_ids=[0])
    return r.results[0]["out_0"][:TOK].reshape(IMGS, NPATCH, D)
```

```python
from contextlib import ExitStack

import concourse.bass as bass
from concourse import mybir

F32 = mybir.dt.float32
BF16 = mybir.dt.bfloat16
I32 = mybir.dt.int32
U32 = mybir.dt.uint32
ALU = mybir.AluOpType
ACT = mybir.ActivationFunctionType
AX = mybir.AxisListType

P = 128
D = 256
KD = D // P
IMGS, NPATCH = 128, 16
TOK = IMGS * NPATCH
NT = TOK // P
IPT = P // NPATCH
NH, HD = 16, 16
HPC = P // HD
FEAT = 768
KF = FEAT // P
PAD = 48
WIN = HD + PAD
EPS = 1e-5
UNROLL = 4
LAG_RANK = 4

E = (8, 9)
HID = (512, 704)
HPAD = (512, 768)
NTILE = tuple(TOK * 2 // P + e - 1 for e in E)
JMAX = max(NTILE)
SLOT = 4352
DUMMY = TOK
ROWS = TOK + P

CONSTS = {}


def _columns():
    at = 0
    for name, n in (("ident", P), ("swap", P), ("upper", P), ("ones", P), ("cos", 16), ("sin", 16),
                    ("mask0", 32), ("mask1", 32), ("block", 8), ("tokid", NT), ("eoff", 9),
                    ("eidx", 9), ("steps", 16), ("tri", 81), ("tile", JMAX), ("nhalf", 1)):
        CONSTS[name] = (at, n)
        at += n
    return at


NCONST = _columns()


def tower(nc, a, tables, out):
    with ExitStack() as ctx:
        def sb(name, shape, dt=F32):
            return ctx.enter_context(nc.sbuf_tensor(name, shape, dt))

        def sem(name):
            return ctx.enter_context(nc.semaphore(name))

        def sem2(name):
            return [sem(f"{name}_{layer}") for layer in range(2)]

        experts = sb("experts", [P, 9 * SLOT])
        consts = sb("consts", [P, NCONST])
        w_qkv = sb("w_qkv", [P, KD, 3 * D])
        w_proj = sb("w_proj", [P, KD, D])
        bias_qk = sb("bias_qk", [P, 4])
        bias_v = sb("bias_v", [P, D])
        bias_proj = sb("bias_proj", [P, D])
        w_gate = sb("w_gate", [P, KD, 9])
        bias_gate = sb("bias_gate", [P, 8])
        h = sb("h", [P, UNROLL, D])
        xln = sb("xln", [P, D])
        turned = sb("turned", [P, 2, KD, P])
        xlnT, xln2T = turned[:, 0], turned[:, 1]
        qk_raw = sb("qk_raw", [P, 4, P])
        rot = sb("rot", [P, 4, P])
        q_sb = sb("q_sb", [P, KD, P])
        k_sb = sb("k_sb", [P, KD, P + PAD])
        v_sb = sb("v_sb", [P, 2, D + PAD])
        spread = sb("spread", [P, 2 * 2 * IPT * P])
        qblk = spread[:, 0:2048].rearrange("p (u g n) -> p u g n", g=HPC, n=16)
        pblk = spread[:, 2048:4096].rearrange("p (g b n) -> p g b n", b=IPT, n=16)
        s_sb = sb("s_sb", [P, 2 * IPT, 16])
        p_sb = sb("p_sb", [P, 2 * IPT, 16])
        s_max = sb("s_max", [P, 2 * IPT])
        s_sum = sb("s_sum", [P, 2 * IPT])
        s_inv = sb("s_inv", [P, 2 * IPT])
        o_sb = sb("o_sb", [P, D])
        oT = sb("oT", [P, KD, P])
        xln2 = sb("xln2", [P, 2, D])
        stats = sb("stats", [P, 2, 6])
        moments = sb("moments", [P, 2, 2])
        var_eps = sb("var_eps", [P, 2])
        rstd = sb("rstd", [P, 2])
        upper_bf = sb("upper_bf", [P, P], BF16)
        ones_bf = sb("ones_bf", [P, P], BF16)
        tok_id = sb("tok_id", [P, NT], I32)
        logits = sb("logits", [P, 9])
        top = sb("top", [P, 8])
        top_i = sb("top_i", [P, 8], U32)
        top_f = sb("top_f", [P, 2])
        gap = sb("gap", [P, 1])
        egap = sb("egap", [P, 1])
        wgt = sb("wgt", [P, 2])
        pick = sb("pick", [P, 2, 9])
        both_bf = sb("both_bf", [P, 9], BF16)
        place = sb("place", [P, 9])
        prod = sb("prod", [P, 9])
        count = sb("count", [P, 9])
        slot_f = sb("slot_f", [P, 2])
        slot_i = sb("slot_i", [P, UNROLL, 2], I32)
        entry = sb("entry", [P, UNROLL, 2, 2], I32)
        tt_n = spread[0:1, 1024:1168].rearrange("p (e i) -> p e i", i=16)
        tt_tiles = spread[0:1, 1168:1177]
        tt_tri = spread[0:1, 1184:1265].rearrange("p (x y) -> p x y", y=9)
        tt_end = spread[0:1, 1280:1289]
        tt_ge = spread[0:1, 0:9 * JMAX].rearrange("p (j e) -> p j e", e=9)
        tt_gt = spread[0:1, 9 * JMAX:18 * JMAX].rearrange("p (j e) -> p j e", e=9)
        tt_e, tt_s, tt_r, tt_r2 = (spread[0:1, at:at + JMAX] for at in (1296, 1344, 1392, 1440))
        tile_row = sb("tile_row", [1, JMAX], I32)
        tile_exp = sb("tile_exp", [1, JMAX], I32)
        places = sb("places", [P, JMAX, 2], I32)
        idx_g = sb("idx_g", [P, 1], I32)
        idx_s = sb("idx_s", [P, 1], I32)
        gate_in = spread[:, 0:512]
        gated = spread[:, 512:1216]
        up_in = spread[:, 1216:1728]
        act = spread[:, 1728:2496]
        actT = spread[:, 2496:3264].rearrange("p (c n) -> p c n", n=P)

        xg = spread[:, 3264:3520]
        xgT = spread[:, 3520:3776].rearrange("p (c n) -> p c n", c=KD)
        y_sb = spread[:, 3776:4032]

        def const(name):
            at, n = CONSTS[name]
            return consts[:, at:at + n]

        tail = experts[:, 8 * SLOT:9 * SLOT]
        w_tok = tail[:, 0:KF * D].rearrange("p (k n) -> p k n", k=KF)
        patch = tail[:, KF * D:KF * D + 2 * FEAT].rearrange("p (s k n) -> p s k n", s=2, k=KF)
        pos = tail[:, KF * D + 2 * FEAT:KF * D + 2 * FEAT + D]
        bias_tok = tail[:, KF * D + 2 * FEAT + D:KF * D + 2 * FEAT + 2 * D]
        by_expert = experts[:, :].rearrange("p (e n) -> p e n", n=SLOT)

        bank = [ctx.enter_context(nc.psum_tensor(f"bank{i}", [P, 512], F32)) for i in range(4)]
        pair45 = ctx.enter_context(nc.psum_tensor("bank45", [P, 2, 512], F32))
        pair67 = ctx.enter_context(nc.psum_tensor("bank67", [P, 2, 512], F32))
        ps_tok, ps_v = bank[0][:, 0:D], bank[0][:, D:2 * D]
        ps_xT, ps_x2T = bank[1][:, 0:D], bank[1][:, D:2 * D]
        ps_qk, ps_swap = bank[2], bank[3]
        ps_sc = pair45[:, :, :]
        ps_pT, ps_proj = bank[3][:, D:2 * D], pair45[:, 1, 0:D]
        ps_o = pair67[:, :, :]
        ps_oT, ps_route, ps_rank = pair67[:, 0, 0:D], pair67[:, 1, 0:9], bank[3][:, 0:32]
        ps_g, ps_u = pair45, pair67
        ps_aT = [bank[0], bank[1]]
        ps_y, ps_gT = bank[2], bank[3]

        consts_in = sem("consts_in")
        small_in = sem2("small_in")
        tokw_in = sem("tokw_in")
        cast_done = sem("cast_done")
        pad_done = sem("pad_done")
        pos_done = sem("pos_done")
        patch_in = [sem("patch_in_even"), sem("patch_in_odd")]
        h_in = [sem(f"h_in_{s}") for s in range(UNROLL)]
        experts_in = sem2("experts_in")
        dummies_in = sem("dummies_in")
        tok_mm = sem("tok_mm")
        h_ready = sem2("h_ready")
        hb_ready = sem2("hb_ready")
        ln_step = sem2("ln_step")
        rstd_ready, rstd2_ready = sem2("rstd_ready"), sem2("rstd2_ready")
        turned_mm, turned_ready = sem2("turned_mm"), sem2("turned_ready")
        qk_mm, qk_ready = sem2("qk_mm"), sem2("qk_ready")
        swap_mm, cos_ready, rot_ready = sem("swap_mm"), sem("cos_ready"), sem("rot_ready")
        rope_done = sem("rope_done")
        qblk_ready = sem2("qblk_ready")
        v_mm, v_ready = sem2("v_mm"), sem2("v_ready")
        sc_mm, sm_step, exp_ready, p_ready = sem2("sc_mm"), sem2("sm_step"), sem2("exp_ready"), sem2("p_ready")
        pT_mm, pblk_ready = sem2("pT_mm"), sem2("pblk_ready")
        o_mm, o_ready = sem2("o_mm"), sem2("o_ready")
        oT_mm, oT_ready = sem2("oT_mm"), sem2("oT_ready")
        proj_mm, h2_ready = sem2("proj_mm"), sem2("h2_ready")
        ln2_step = sem2("ln2_step")
        h2_out = [[sem(f"h2_out_{layer}_{s}") for s in range(UNROLL)] for layer in range(2)]
        xln2_out = [[sem(f"xln2_out_{layer}_{s}") for s in range(2)] for layer in range(2)]
        route_mm, rt_step, egap_ready = sem2("route_mm"), sem2("rt_step"), sem2("egap_ready")
        rank_mm, entry_ready, entry_out = sem2("rank_mm"), sem2("entry_ready"), sem2("entry_out")
        slot_step, wgt_in = sem2("slot_step"), sem2("wgt_in")
        tt_step, tt_sum = sem2("tt_step"), sem2("tt_sum")
        count_zero, act_pad, w_pad = sem("count_zero"), sem("act_pad"), sem("w_pad")
        waited = sem("waited")
        places_in = [[sem(f"places_in_{layer}_{s}") for s in ("0", "1", "2", "rest")] for layer in range(2)]
        idx_g_ready, gather_in = sem2("idx_g_ready"), sem2("gather_in")
        gT_mm, gT_ready = sem2("gT_mm"), sem2("gT_ready")
        g_mm, u_mm = sem2("g_mm"), sem2("u_mm")
        gbias_ready, ubias_ready, silu_ready, act_ready = sem2("gbias_ready"), sem2("ubias_ready"), sem2("silu_ready"), sem2("act_ready")
        aT_mm, aT_ready = sem2("aT_mm"), sem2("aT_ready")
        y_mm, yb_ready, y_ready = sem2("y_mm"), sem2("yb_ready"), sem2("y_ready")
        idx_s_ready, added = sem2("idx_s_ready"), sem2("added")

        N_CONST = 16
        SMALL = 6 * 16
        LN_STEPS = 4
        SM_STEPS = 6
        RT_STEPS = 14
        BLK = HPC
        TT_STEPS = 11
        W_DMAS = (4 * E[0] * 16, 4 * E[1] * 16)
        RESID = [tables["resid"], out]
        NORMED = [tables["normed0"], tables["normed1"]]
        TABLE = [tables["table0"], tables["table1"]]

        def steps(engine, step):
            total = NT + LAG_RANK
            for i in range(UNROLL):
                step(i, i)
            with engine.Fori(1, NT // UNROLL) as group:
                for d in range(UNROLL):
                    step(group * UNROLL + d, d)
            for i in range(NT, total):
                step(i, i % UNROLL)

        def live(i, lag):
            return not isinstance(i, int) or 0 <= i - lag < NT

        def wait_turn(engine, semaphores, i, d, lag):
            n = len(semaphores)
            at = d - lag
            if live(i, lag):
                if isinstance(i, int):
                    engine.wait_ge(semaphores[at % n], 16 * ((i - lag) // n + 1))
                else:
                    engine.wait_ge(semaphores[at % n], (i - d) * (16 // n) + 16 * (at // n + 1))

        def wait(engine, semaphore, value):
            if not isinstance(value, int) or value > 0:
                engine.wait_ge(semaphore, value)

        def apart(engine):
            engine.sem_inc(waited, 1)

        def in_heads(x, part):
            return x[:, 2 * part:2 * part + 2].rearrange("p c (b n) -> p (c b) n", n=NPATCH)

        def rotary(name):
            return const(name).unsqueeze(1).to_broadcast([P, KD * IPT, NPATCH])

        block = ctx.enter_context(nc.Block())

        @block.sync
        def _(sp):
            sp.dma_start(consts[:], a["consts"]).then_inc(consts_in, N_CONST)
            sp.dma_start(w_tok, a["w_tok"]).then_inc(tokw_in, 16)
            sp.dma_start(pos, a["pos"]).then_inc(tokw_in, 16)
            sp.dma_start(bias_tok, a["b_tok"].partition_broadcast(P)).then_inc(tokw_in, 16)

            def small(layer):
                sp.dma_start(w_qkv[:], a[f"w_qkv{layer}"]).then_inc(small_in[layer], 16)
                sp.dma_start(bias_qk[:], a[f"b_qk{layer}"]).then_inc(small_in[layer], 16)
                sp.dma_start(bias_v[:], a[f"b_v{layer}"].partition_broadcast(P)).then_inc(small_in[layer], 16)
                sp.dma_start(bias_proj[:], a[f"b_proj{layer}"].partition_broadcast(P)).then_inc(small_in[layer], 16)
                sp.dma_start(w_proj[:], a[f"w_proj{layer}"]).then_inc(small_in[layer], 16)
                sp.dma_start(w_gate[:, :, 0:E[layer]], a[f"w_gate{layer}"]).then_inc(small_in[layer], 16)
                if layer == 0:
                    sp.dma_start(bias_gate[:], a["b_gate"].partition_broadcast(P)).then_inc(small_in[0], 16)

            def attention(layer):
                def step(i, d):
                    if layer == 0 and live(i, 0):
                        wait(sp, tok_mm, i - 1)
                        sp.dma_start(patch[:, d % 2], a["patches"][bass.ts(i, P), :].rearrange("p (k n) -> p k n", k=KF)).then_inc(patch_in[d % 2], 16)
                        if isinstance(i, int) and i == 1:
                            small(0)
                            for table, n in ((0, E[0]), (1, E[1])):
                                sp.dma_start(TABLE[table], a[f"empty{table}"]).then_inc(dummies_in, 16)
                            for rows in (RESID[0], NORMED[0], NORMED[1], RESID[1]):
                                sp.dma_start(rows[DUMMY:ROWS, :], a["zeros"]).then_inc(dummies_in, 16)
                    if layer == 1 and live(i, 0):
                        wait_turn(sp, h2_out[1], i, d, 4)
                        apart(sp)
                        wait(sp, ln2_step[1], LN_STEPS * (i - 3))
                        sp.dma_start(h[:, d], RESID[0][bass.ts(i, P), :]).then_inc(h_in[d], 16)
                    if live(i, 3):
                        wait(sp, h2_ready[layer], i - 2)
                        sp.dma_start(RESID[layer][bass.ts(i - 3, P), :], h[:, (d - 3) % UNROLL]).then_inc(h2_out[layer][(d - 3) % UNROLL], 16)
                        wait(sp, ln2_step[layer], LN_STEPS * (i - 2))
                        sp.dma_start(NORMED[layer][bass.ts(i - 3, P), :], xln2[:, (d - 3) % 2]).then_inc(xln2_out[layer][(d - 3) % 2], 16)
                steps(sp, step)

            def moe(layer):
                sp.wait_ge(tt_step[layer], TT_STEPS)
                sp.wait_ge(entry_out[layer], 32 * NT)
                if layer == 1:
                    sp.wait_ge(idx_s_ready[0], NTILE[0])
                    sp.wait_ge(y_ready[0], NTILE[0])

                def load(j, done):
                    row = sp.value_load(tile_row[0:1, bass.ds(j, 1)], min_val=0, max_val=(E[layer] + 1) * TOK - P)
                    sp.dma_start(places[:, bass.ds(j, 1), :], TABLE[layer][bass.ds(row, P), :].rearrange("p (o n) -> p o n", o=1)).then_inc(done, 16)

                for j in range(3):
                    load(j, places_in[layer][j])
                with sp.Fori(3, NTILE[layer]) as j:
                    load(j, places_in[layer][3])

            attention(0)
            moe(0)
            sp.wait_ge(added[0], 16 * NTILE[0])
            sp.wait_ge(proj_mm[0], NT)
            small(1)
            attention(1)
            moe(1)
            for stored in h2_out[1]:
                sp.wait_ge(stored, 16 * NT // UNROLL)
            sp.wait_ge(dummies_in, 6 * 16)
            sp.wait_ge(added[1], 16 * NTILE[1])

        @block.gpsimd
        def _(pool):
            nc.gpsimd.memset(k_sb[:, :, P:P + PAD], 0.0).then_inc(pad_done, 1)
            nc.gpsimd.memset(v_sb[:, :, D:D + PAD], 0.0).then_inc(pad_done, 1)
            pool.wait_ge(consts_in, N_CONST)
            nc.gpsimd.tensor_copy(upper_bf[:], const("upper")).then_inc(cast_done, 1)
            nc.gpsimd.tensor_copy(ones_bf[:], const("ones")).then_inc(cast_done, 1)
            nc.gpsimd.tensor_copy(tok_id[:], const("tokid")).then_inc(cast_done, 1)
            pool.wait_ge(tokw_in, 48)
            nc.gpsimd.tensor_tensor(pos, pos, bias_tok, ALU.add).then_inc(pos_done, 1)

            def attention(layer):
                def step(i, d):
                    if live(i, 3):
                        wait(pool, ln2_step[layer], LN_STEPS * (i - 3) + 3)
                        nc.gpsimd.tensor_tensor(rstd[:, 1:2], var_eps[:, 1:2], const("nhalf"), ALU.pow).then_inc(rstd2_ready[layer], 1)
                    if live(i, 0):
                        wait(pool, ln_step[layer], LN_STEPS * i + 3)
                        nc.gpsimd.tensor_tensor(rstd[:, 0:1], var_eps[:, 0:1], const("nhalf"), ALU.pow).then_inc(rstd_ready[layer], 1)
                        if isinstance(i, int) and i == 0:
                            pool.wait_ge(small_in[layer], SMALL + 16 * (1 - layer))
                        wait(pool, ln_step[layer], LN_STEPS * (i + 1))
                        nc.gpsimd.tensor_tensor(h[:, d], h[:, d], bias_proj[:], ALU.add).then_inc(hb_ready[layer], 1)
                    if live(i, 4):
                        wait(pool, entry_ready[layer], i - 3)
                        for c in range(2):
                            apart(pool)
                            nc.gpsimd.indirect_dma_start(
                                out=TABLE[layer], out_offset=bass.IndirectOffsetOnAxis(slot_i[:, d, c:c + 1], 0),
                                in_=entry[:, d, c], in_offset=None).then_inc(entry_out[layer], 16)
                    if layer == 1 and live(i, 0):
                        for part in range(2):
                            wait(pool, qk_ready[1], 4 * i + 2 * part + 2)
                            nc.gpsimd.tensor_tensor(in_heads(rot, part), in_heads(qk_raw, part), rotary("cos"), ALU.mult).then_inc(cos_ready, 1)
                    if live(i, 4):
                        wait(pool, entry_out[layer], 32 * (i - 3))
                steps(pool, step)

            def moe(layer):
                n = NTILE[layer]
                for stored in xln2_out[layer] + h2_out[layer]:
                    pool.wait_ge(stored, 16 * NT // (2 if stored in xln2_out[layer] else UNROLL))

                def gather(j):
                    if isinstance(j, int) and j < 3:
                        pool.wait_ge(places_in[layer][j], 16)
                    else:
                        pool.wait_ge(places_in[layer][3], 16 * (n - 3))
                    wait(pool, gather_in[layer], 16 * j)
                    nc.gpsimd.tensor_copy(idx_g[:], places[:, bass.ds(j, 1), 0]).then_inc(idx_g_ready[layer], 1)
                    wait(pool, gT_mm[layer], j)
                    pool.wait_ge(idx_g_ready[layer], j + 1)
                    apart(pool)
                    nc.gpsimd.indirect_dma_start(out=xg, out_offset=None, in_=NORMED[layer],
                                                 in_offset=bass.IndirectOffsetOnAxis(idx_g[:, 0:1], 0)).then_inc(gather_in[layer], 16)

                def add(j):
                    wait(pool, added[layer], 16 * j)
                    nc.gpsimd.tensor_copy(idx_s[:], places[:, bass.ds(j, 1), 0]).then_inc(idx_s_ready[layer], 1)
                    pool.wait_ge(y_ready[layer], j + 1)
                    pool.wait_ge(idx_s_ready[layer], j + 1)
                    apart(pool)
                    nc.gpsimd.indirect_dma_start(out=RESID[layer], out_offset=bass.IndirectOffsetOnAxis(idx_s[:, 0:1], 0),
                                                 in_=y_sb, in_offset=None, compute_op=ALU.add).then_inc(added[layer], 16)

                for j in range(4):
                    gather(j)
                add(0)
                with pool.Fori(4, n) as j:
                    gather(j)
                    add(j - 3)
                for j in range(n - 3, n):
                    add(j)

            pool.wait_ge(dummies_in, 6 * 16)
            for layer in range(2):
                if layer == 1:
                    pool.wait_ge(y_mm[0], NTILE[0])
                    nc.gpsimd.memset(by_expert[64:P, :, SLOT - D:SLOT], 0.0).then_inc(w_pad, 1)
                    pool.wait_ge(w_pad, 1)
                attention(layer)
                moe(layer)

        @block.scalar
        def _(act_e):
            def load_experts(layer):
                for e in range(E[layer]):
                    slot = by_expert[:, e]
                    at = 0
                    for name, n in ((("w_up0", 1024), ("w_gate_h0", 1024), ("w_down0", 1024)) if layer == 0 else
                                    (("w_gate_h1", 1408), ("w_up1", 1408))):
                        act_e.dma_start(slot[:, at:at + n], a[name][e]).then_inc(experts_in[layer], 16)
                        at += n
                    if layer == 0:
                        act_e.dma_start(slot[:, at:at + 1280], a["b_exp"][e:e + 1, :].partition_broadcast(P)).then_inc(experts_in[0], 16)
                    else:
                        act_e.dma_start(slot[:, at:at + 1280].rearrange("p (k n) -> p k n", n=D), a["w_down1"][e, 0:640, :].rearrange("(k p) n -> p k n", p=P)).then_inc(experts_in[1], 16)
                        act_e.dma_start(slot[0:64, at + 1280:at + 1536], a["w_down1"][e, 640:704, :]).then_inc(experts_in[1], 16)

            def attention(layer):
                def take_heads(t, s):
                    wait(act_e, o_mm[layer], 2 * t + s + 1)
                    nc.scalar.activation(o_sb[:, s * P:(s + 1) * P].rearrange("p (g n) -> p g n", n=HD),
                                         ps_o[:, s].rearrange("p (g w) -> p g w", w=WIN)[:, :, 0:HD], ACT.Copy).then_inc(o_ready[layer], 1)

                def step(i, d):
                    if live(i, 0) or live(i, 3):
                        wait(act_e, turned_mm[layer], i + 1)
                        if live(i, 0):
                            wait(act_e, v_mm[layer], i)
                        if live(i, 3):
                            wait(act_e, route_mm[layer], i - 3)
                        lo, hi = 0 if live(i, 0) else 1, 2 if live(i, 3) else 1
                        nc.scalar.activation(turned[:, lo:hi].rearrange("p s c n -> p (s c n)"), bank[1][:, lo * D:hi * D], ACT.Copy).then_inc(turned_ready[layer], 1)
                    if live(i, 1):
                        wait(act_e, sm_step[layer], SM_STEPS * (i - 1) + 4)
                        nc.scalar.activation(s_sb[:], s_sb[:], ACT.Exp).then_inc(exp_ready[layer], 1)
                    if live(i, 2):
                        wait(act_e, oT_mm[layer], i - 2)
                        take_heads(i - 2, 0)
                    if live(i, 0):
                        if layer == 0:
                            wait(act_e, qblk_ready[0], BLK * i)
                            wait(act_e, sc_mm[0], 2 * i)
                        else:
                            wait(act_e, rope_done, 2 * i)
                        if isinstance(i, int) and i == 0:
                            act_e.wait_ge(small_in[layer], SMALL + 16 * (1 - layer))
                            act_e.wait_ge(pad_done, 2)
                        wait(act_e, qk_mm[layer], i + 1)
                        for c in range(4):
                            to = qk_raw[:, c] if layer else (q_sb[:, c] if c < 2 else k_sb[:, c - 2, 0:P])
                            nc.scalar.activation(to, ps_qk[:, c * P:(c + 1) * P], ACT.Identity, bias=bias_qk[:, c:c + 1]).then_inc(qk_ready[layer], 1)
                    if live(i, 3):
                        wait(act_e, rt_step[layer], RT_STEPS * (i - 3) + 4)
                        nc.scalar.activation(egap[:], gap[:], ACT.Exp).then_inc(egap_ready[layer], 1)
                    if live(i, 2):
                        take_heads(i - 2, 1)
                        wait(act_e, oT_mm[layer], i - 1)
                        wait(act_e, proj_mm[layer], i - 2)
                        nc.scalar.activation(oT[:].rearrange("p c n -> p (c n)"), ps_oT, ACT.Copy).then_inc(oT_ready[layer], 1)
                    if live(i, 1):
                        wait(act_e, pT_mm[layer], i)
                        wait(act_e, o_mm[layer], 2 * (i - 1))
                        for b in range(IPT):
                            nc.scalar.activation(pblk[:, :, b], ps_pT.rearrange("p (g n) -> p g n", n=16), ACT.Copy, scale=const("block")[:, b:b + 1]).then_inc(pblk_ready[layer], 1)
                steps(act_e, step)

            def moe(layer):
                n = NTILE[layer]
                hid = HID[layer]
                gv = gated[:, 0:hid] if layer == 0 else gated[:, 0:hid].rearrange("p (s n) -> p s n", s=2)

                def gate(j):
                    wait(act_e, act_ready[layer], j)
                    if layer == 0:
                        act_e.wait_ge(gbias_ready[0], j + 1)
                        nc.scalar.activation(gv, gate_in, ACT.Silu).then_inc(silu_ready[0], 1)
                    else:
                        act_e.wait_ge(g_mm[1], j + 1)
                        nc.scalar.activation(gv, ps_g[:, :, 0:hid // 2], ACT.Silu).then_inc(silu_ready[1], 1)

                def turned_in(j):
                    act_e.wait_ge(gT_mm[layer], j + 1)
                    nc.scalar.activation(xgT.rearrange("p c n -> p (c n)"), ps_gT[:, 0:D], ACT.Copy).then_inc(gT_ready[layer], 1)

                def turned(j):
                    act_e.wait_ge(aT_mm[layer], j + 1)
                    half = actT.rearrange("p c n -> p (c n)")
                    nc.scalar.activation(half[:, 0:512], ps_aT[0][:, 0:512], ACT.Copy).then_inc(aT_ready[layer], 1)
                    if layer == 1:
                        nc.scalar.activation(half[:, 512:768], ps_aT[1][:, 0:256], ACT.Copy).then_inc(aT_ready[1], 1)

                turned_in(0)
                gate(0)
                turned_in(1)
                with act_e.Fori(1, n - 1) as j:
                    gate(j)
                    turned(j - 1)
                    turned_in(j + 1)
                gate(n - 1)
                turned(n - 2)
                turned(n - 1)

            load_experts(0)
            attention(0)
            moe(0)
            act_e.wait_ge(y_mm[0], NTILE[0])
            act_e.wait_ge(yb_ready[0], NTILE[0])
            load_experts(1)
            attention(1)
            moe(1)

        @block.vector
        def _(dve):
            def layer_norms(*norms):
                for x, to, slot, done, inverse, i in norms:
                    nc.vector.bn_stats(stats[:, slot], x).then_inc(done, 1)
                for x, to, slot, done, inverse, i in norms:
                    dve.wait_ge(done, LN_STEPS * i + 1)
                    apart(dve)
                    nc.vector.bn_aggr(moments[:, slot], stats[:, slot]).then_inc(done, 1)
                for x, to, slot, done, inverse, i in norms:
                    dve.wait_ge(done, LN_STEPS * i + 2)
                    nc.vector.tensor_scalar(var_eps[:, slot:slot + 1], moments[:, slot, 1:2], EPS, None, ALU.add).then_inc(done, 1)
                for x, to, slot, done, inverse, i in norms:
                    dve.wait_ge(inverse, i + 1)
                    nc.vector.tensor_scalar(to, x, moments[:, slot, 0:1], rstd[:, slot:slot + 1], ALU.subtract, ALU.mult).then_inc(done, 1)

            def softmax(layer, t, meanwhile):
                s = SM_STEPS * t
                step_sem = sm_step[layer]
                mask = const(f"mask{layer}").rearrange("p (c k) -> p c k", c=2)
                for c in range(2):
                    dve.wait_ge(sc_mm[layer], 2 * t + c + 1)
                    nc.vector.scalar_tensor_tensor(
                        s_sb[:, c * IPT:(c + 1) * IPT], ps_sc[:, c].rearrange("p (b w) -> p b w", w=WIN)[:, :, 0:16], float(HD) ** -0.5,
                        mask[:, c:c + 1, :].to_broadcast([P, IPT, 16]), ALU.mult, ALU.add).then_inc(step_sem, 1)
                dve.wait_ge(step_sem, s + 2)
                nc.vector.tensor_reduce(s_max[:], s_sb[:], AX.X, ALU.max).then_inc(step_sem, 1)
                dve.wait_ge(step_sem, s + 3)
                nc.vector.tensor_tensor(s_sb[:], s_sb[:], s_max[:].unsqueeze(2).to_broadcast([P, 16, 16]), ALU.subtract).then_inc(step_sem, 1)
                meanwhile()
                dve.wait_ge(exp_ready[layer], t + 1)
                nc.vector.tensor_reduce(s_sum[:], s_sb[:], AX.X, ALU.add).then_inc(step_sem, 1)
                dve.wait_ge(step_sem, s + 5)
                nc.vector.reciprocal(s_inv[:], s_sum[:]).then_inc(step_sem, 1)
                dve.wait_ge(step_sem, s + 6)
                wait(dve, pT_mm[layer], t)
                nc.vector.tensor_tensor(p_sb[:], s_sb[:], s_inv[:].unsqueeze(2).to_broadcast([P, 16, 16]), ALU.mult).then_inc(p_ready[layer], 1)

            def route(layer, t):
                e = E[layer]
                s = RT_STEPS * t
                st = rt_step[layer]
                dve.wait_ge(route_mm[layer], t + 1)
                if layer == 0:
                    nc.vector.tensor_tensor(logits[:, 0:e], ps_route[:, 0:e], bias_gate[:], ALU.add).then_inc(st, 1)
                else:
                    nc.vector.tensor_copy(logits[:, 0:e], ps_route[:, 0:e]).then_inc(st, 1)
                dve.wait_ge(st, s + 1)
                apart(dve)
                nc.vector.max(top[:], logits[:, 0:e]).then_inc(st, 1)
                dve.wait_ge(st, s + 2)
                apart(dve)
                nc.vector.max_index(top_i[:], top[:], logits[:, 0:e]).then_inc(st, 1)
                nc.vector.tensor_tensor(gap[:], top[:, 1:2], top[:, 0:1], ALU.subtract).then_inc(st, 1)
                dve.wait_ge(st, s + 4)
                nc.vector.tensor_copy(top_f[:], top_i[:, 0:2]).then_inc(st, 1)
                dve.wait_ge(st, s + 5)
                for c in range(2):
                    nc.vector.tensor_scalar(pick[:, c, 0:e], const("eidx")[:, 0:e], top_f[:, c:c + 1], None, ALU.is_equal).then_inc(st, 1)
                dve.wait_ge(st, s + 7)
                nc.vector.tensor_tensor(both_bf[:, 0:e], pick[:, 0, 0:e], pick[:, 1, 0:e], ALU.add).then_inc(st, 1)

            def entries(layer, t, slot):
                e = E[layer]
                s = RT_STEPS * t
                st = rt_step[layer]
                dve.wait_ge(egap_ready[layer], t + 1)
                nc.vector.tensor_scalar(wgt[:, 1:2], egap[:], 1.0, None, ALU.add).then_inc(st, 1)
                dve.wait_ge(rank_mm[layer], t + 1)
                nc.vector.tensor_tensor(place[:, 0:e], ps_rank[:, 0:e], count[:, 0:e], ALU.add).then_inc(st, 1)
                dve.wait_ge(st, s + 9)
                nc.vector.reciprocal(wgt[:, 0:1], wgt[:, 1:2]).then_inc(st, 1)
                dve.wait_ge(st, s + 10)
                nc.vector.tensor_tensor(count[:, 0:e], count[:, 0:e], ps_rank[:, 16:16 + e], ALU.add).then_inc(st, 1)
                dve.wait_ge(st, s + 11)
                nc.vector.tensor_tensor(wgt[:, 1:2], wgt[:, 0:1], egap[:], ALU.mult).then_inc(st, 1)
                nc.vector.tensor_tensor(place[:, 0:e], place[:, 0:e], const("eoff")[:, 0:e], ALU.add).then_inc(st, 1)
                dve.wait_ge(st, s + 14)

                for c in range(2):
                    nc.vector.tensor_tensor_reduce(prod[:, 0:e], pick[:, c, 0:e], place[:, 0:e], 1.0, 0.0, ALU.mult, ALU.add,
                                                   slot_f[:, c:c + 1]).then_inc(slot_step[layer], 1)
                    dve.wait_ge(slot_step[layer], 3 * t + c + 1)
                nc.vector.tensor_copy(slot_i[:, slot], slot_f[:]).then_inc(slot_step[layer], 1)
                dve.wait_ge(slot_step[layer], 3 * t + 3)
                nc.vector.tensor_copy(entry[:, slot, :, 1].bitcast(F32), wgt[:]).then_inc(wgt_in[layer], 1)
                dve.wait_ge(wgt_in[layer], t + 1)
                nc.vector.tensor_copy(entry[:, slot, :, 0], tok_id[:, bass.ds(t, 1)].to_broadcast([P, 2])).then_inc(entry_ready[layer], 1)

            def attention(layer):
                def spread_queries(i):
                    wait(dve, sc_mm[layer], 2 * i)
                    for g in range(HPC):
                        nc.vector.tensor_scalar(qblk[:, :, g], q_sb[:].rearrange("p c (b n) -> p (c b) n", n=16), const("block")[:, g:g + 1], None, ALU.mult).then_inc(qblk_ready[layer], 1)

                def step(i, d):
                    second, first = [], []
                    if live(i, 3):
                        wait(dve, proj_mm[layer], i - 2)
                        wait(dve, hb_ready[layer], i - 2)
                        hh = h[:, (d - 3) % UNROLL]
                        nc.vector.tensor_tensor(hh, ps_proj, hh, ALU.add).then_inc(h2_ready[layer], 1)
                        wait(dve, h2_ready[layer], i - 2)
                        wait_turn(dve, xln2_out[layer], i, d, 5)
                        if layer == 0 or not live(i, 0):
                            wait(dve, turned_mm[layer], i - 1)
                        second = [(hh, xln2[:, (d - 3) % 2], 1, ln2_step[layer], rstd2_ready[layer], i - 3)]
                    if live(i, 0):
                        first = [(h[:, d], xln[:], 0, ln_step[layer], rstd_ready[layer], i)]
                        if layer == 0:
                            if second:
                                layer_norms(*second)
                                second = []
                            wait(dve, tok_mm, i + 1)
                            wait_turn(dve, h2_out[0], i, d, 4)
                            wait(dve, ln2_step[0], LN_STEPS * (i - 3))
                            nc.vector.tensor_tensor(h[:, d], ps_tok, pos, ALU.add).then_inc(h_ready[0], 1)
                            dve.wait_ge(h_ready[0], i + 1)
                        elif isinstance(i, int):
                            dve.wait_ge(h_in[d], 16 * (i // UNROLL + 1))
                        else:
                            dve.wait_ge(h_in[d], (i - d) * (16 // UNROLL) + 16)
                        wait(dve, turned_mm[layer], i)
                    layer_norms(*second, *first)
                    if live(i, 1):
                        softmax(layer, i - 1, lambda: entries(layer, i - 4, d) if live(i, 4) else None)
                    elif live(i, 4):
                        entries(layer, i - 4, d)
                    if live(i, 3):
                        route(layer, i - 3)
                    if live(i, 0) and layer == 0:
                        wait(dve, qk_ready[0], 4 * i + 2)
                        spread_queries(i)
                    if live(i, 0) and layer == 1:
                        for part in range(2):
                            wait(dve, cos_ready, 2 * i + part + 1)
                            wait(dve, swap_mm, i + 1)
                            nc.vector.tensor_tensor(in_heads(qk_raw, part), ps_swap[:, part * D:(part + 1) * D].rearrange("p (b n) -> p b n", n=NPATCH),
                                                    rotary("sin"), ALU.mult).then_inc(rot_ready, 1)
                            wait(dve, rot_ready, 2 * i + part + 1)
                            wait(dve, sc_mm[1], 2 * i)
                            to = q_sb[:] if part == 0 else k_sb[:, :, 0:P]
                            nc.vector.tensor_tensor(to, rot[:, 2 * part:2 * part + 2], qk_raw[:, 2 * part:2 * part + 2], ALU.add).then_inc(rope_done, 1)
                        wait(dve, rope_done, 2 * i + 1)
                        spread_queries(i)
                    if live(i, 0):
                        if isinstance(i, int) and i == 0:
                            dve.wait_ge(small_in[layer], SMALL + 16 * (1 - layer))
                        wait(dve, v_mm[layer], i + 1)
                        wait(dve, o_mm[layer], 2 * (i - 1))
                        nc.vector.tensor_tensor(v_sb[:, d % 2, 0:D], ps_v, bias_v[:], ALU.add).then_inc(v_ready[layer], 1)
                steps(dve, step)

            def tile_table(layer):
                e, n, st = E[layer], NTILE[layer], tt_step[layer]
                dve.wait_ge(slot_step[layer], 3 * NT)
                cnt = count[0:1, 0:e]
                row = lambda name, m: const(name)[0:1, 0:m]
                nc.vector.tensor_tensor(tt_n[:, 0:e], cnt.unsqueeze(2).to_broadcast([1, e, 16]), row("steps", 16).unsqueeze(1).to_broadcast([1, e, 16]), ALU.is_gt).then_inc(st, 1)
                dve.wait_ge(st, 1)
                nc.vector.tensor_reduce(tt_tiles[:, 0:e], tt_n[:, 0:e], AX.X, ALU.add).then_inc(st, 1)
                dve.wait_ge(st, 2)
                tri = row("tri", 81).rearrange("p (x y) -> p x y", y=9)[:, 0:e, 0:e]
                nc.vector.tensor_tensor(tt_tri[:, 0:e, 0:e], tt_tiles[:, 0:e].unsqueeze(1).to_broadcast([1, e, e]), tri, ALU.mult).then_inc(st, 1)
                dve.wait_ge(st, 3)
                nc.vector.tensor_reduce(tt_end[:, 0:e], tt_tri[:, 0:e, 0:e], AX.X, ALU.add).then_inc(st, 1)
                dve.wait_ge(st, 4)
                nc.vector.tensor_tensor(tt_ge[:, 0:n, 0:e], row("tile", n).unsqueeze(2).to_broadcast([1, n, e]), tt_end[:, 0:e].unsqueeze(1).to_broadcast([1, n, e]), ALU.is_ge).then_inc(st, 1)
                dve.wait_ge(st, 5)
                nc.vector.tensor_reduce(tt_e[:, 0:n], tt_ge[:, 0:n, 0:e], AX.X, ALU.add).then_inc(st, 1)
                nc.vector.tensor_tensor(tt_gt[:, 0:n, 0:e], tt_ge[:, 0:n, 0:e], tt_tiles[:, 0:e].unsqueeze(1).to_broadcast([1, n, e]), ALU.mult).then_inc(st, 1)
                dve.wait_ge(st, 7)
                nc.vector.tensor_reduce(tt_s[:, 0:n], tt_gt[:, 0:n, 0:e], AX.X, ALU.add).then_inc(st, 1)
                nc.vector.tensor_scalar(tile_exp[:, 0:n], tt_e[:, 0:n], float(e - 1), None, ALU.min).then_inc(st, 1)
                dve.wait_ge(st, 8)
                nc.vector.tensor_tensor(tt_r[:, 0:n], row("tile", n), tt_s[:, 0:n], ALU.subtract).then_inc(st, 1)
                dve.wait_ge(st, 10)
                nc.vector.scalar_tensor_tensor(tt_r2[:, 0:n], tt_e[:, 0:n], float(TOK // P), tt_r[:, 0:n], ALU.mult, ALU.add).then_inc(tt_sum[layer], 1)
                dve.wait_ge(tt_sum[layer], 1)
                nc.vector.tensor_scalar(tile_row[:, 0:n], tt_r2[:, 0:n], float(P), None, ALU.mult).then_inc(st, 1)

            def moe(layer):
                n, hid = NTILE[layer], HID[layer]
                half = hid // 2
                if layer == 1:
                    dve.wait_ge(tt_step[1], TT_STEPS)
                    nc.vector.memset(act[:, hid:HPAD[1]], 0.0).then_inc(act_pad, 1)
                else:
                    dve.wait_ge(experts_in[0], W_DMAS[0])

                def expert_of(j):
                    return dve.value_load(tile_exp[0:1, bass.ds(j, 1)], min_val=0, max_val=E[layer] - 1)

                def bias(e, at, m):
                    return experts[:, bass.ds(e * SLOT + 3072 + at, m)]

                def hidden(j, e):
                    if layer == 0:
                        dve.wait_ge(g_mm[0], j + 1)
                        wait(dve, silu_ready[0], j)
                        nc.vector.tensor_tensor(gate_in, ps_g[:, 0], bias(e, 512, 512), ALU.add).then_inc(gbias_ready[0], 1)
                        dve.wait_ge(u_mm[0], j + 1)
                        nc.vector.tensor_tensor(up_in, ps_u[:, 0], bias(e, 0, 512), ALU.add).then_inc(ubias_ready[0], 1)
                        dve.wait_ge(ubias_ready[0], j + 1)
                        dve.wait_ge(silu_ready[0], j + 1)
                        nc.vector.tensor_tensor(act[:, 0:hid], up_in, gated[:, 0:hid], ALU.mult).then_inc(act_ready[0], 1)
                    else:
                        dve.wait_ge(u_mm[1], j + 1)
                        dve.wait_ge(silu_ready[1], j + 1)
                        nc.vector.tensor_tensor(act[:, 0:hid].rearrange("p (s n) -> p s n", s=2), ps_u[:, :, 0:half],
                                                gated[:, 0:hid].rearrange("p (s n) -> p s n", s=2), ALU.mult).then_inc(act_ready[1], 1)

                def weighted(j, e):
                    dve.wait_ge(y_mm[layer], j + 1)
                    wait(dve, added[layer], 16 * j)
                    w = places[:, bass.ds(j, 1), 1].bitcast(F32)
                    if layer == 0:
                        nc.vector.tensor_tensor(y_sb, ps_y[:, 0:D], bias(e, 1024, D), ALU.add).then_inc(yb_ready[0], 1)
                        dve.wait_ge(yb_ready[0], j + 1)
                        nc.vector.tensor_scalar(y_sb, y_sb, w, None, ALU.mult).then_inc(y_ready[0], 1)
                    else:
                        nc.vector.tensor_scalar(y_sb, ps_y[:, 0:D], w, None, ALU.mult).then_inc(y_ready[1], 1)

                hidden(0, expert_of(0))
                with dve.Fori(1, n) as j:
                    hidden(j, expert_of(j))
                    weighted(j - 1, expert_of(j - 1))
                weighted(n - 1, expert_of(n - 1))

            dve.wait_ge(consts_in, N_CONST)
            dve.wait_ge(cast_done, 3)
            dve.wait_ge(pos_done, 1)
            for layer in range(2):
                nc.vector.memset(count[:], 0.0).then_inc(count_zero, 1)
                dve.wait_ge(count_zero, layer + 1)
                attention(layer)
                tile_table(layer)
                moe(layer)

        @block.tensor
        def _(pe):
            ident = const("ident")

            def attention(layer):
                def attend(lo, hi, d):
                    for g in range(lo, hi):
                        mm = nc.tensor.matmul(ps_o[:, g // 8, (g % 8) * WIN:(g % 8 + 1) * WIN],
                                              pblk[:, g].rearrange("p b n -> p (b n)"),
                                              v_sb[:, d % 2, g * HD:g * HD + WIN], start=True, stop=True)
                    return mm

                def step(i, d):
                    if layer == 0 and live(i, 0):
                        if isinstance(i, int):
                            pe.wait_ge(patch_in[d % 2], 16 * (i // 2 + 1))
                        else:
                            pe.wait_ge(patch_in[d % 2], (i - d) * 8 + 16 * (d // 2 + 1))
                        wait(pe, v_ready[0], i)
                        for k in range(KF):
                            mm = nc.tensor.matmul(ps_tok, patch[:, d % 2, k], w_tok[:, k], start=k == 0, stop=k == KF - 1)
                        mm.then_inc(tok_mm, 1)
                    if live(i, 1):
                        wait(pe, qblk_ready[layer], BLK * i)
                        wait(pe, qk_ready[layer], 4 * i)
                        if layer == 1:
                            wait(pe, rope_done, 2 * i)
                        for c in range(KD):
                            if c == 1:
                                wait(pe, h2_ready[layer], i - 2)
                            for b in range(IPT):
                                mm = nc.tensor.matmul(ps_sc[:, c, b * WIN:(b + 1) * WIN], qblk[:, c * IPT + b].rearrange("p g n -> p (g n)"),
                                                      k_sb[:, c, b * 16:b * 16 + WIN], start=True, stop=True)
                            mm.then_inc(sc_mm[layer], 1)
                    if live(i, 4):
                        e = E[layer]
                        wait(pe, rt_step[layer], RT_STEPS * (i - 4) + 8)
                        wait(pe, pblk_ready[layer], BLK * min(i - 1, NT) if isinstance(i, int) else BLK * (i - 1))
                        if layer == 1:
                            wait(pe, rot_ready, 2 * min(i, NT) if isinstance(i, int) else 2 * i)
                        nc.tensor.matmul(ps_rank[:, 0:e], upper_bf[:], both_bf[:, 0:e], start=True, stop=True)
                        mm = nc.tensor.matmul(ps_rank[:, 16:16 + e], ones_bf[:], both_bf[:, 0:e], start=True, stop=True)
                        mm.then_inc(rank_mm[layer], 1)
                    if live(i, 0) or live(i, 3):
                        wait(pe, turned_ready[layer], i)
                        if live(i, 0):
                            wait(pe, ln_step[layer], LN_STEPS * (i + 1))
                            for c in range(KD):
                                mm = nc.tensor.transpose(ps_xT[:, c * P:(c + 1) * P], xln[:, c * P:(c + 1) * P], ident)
                        if live(i, 3):
                            wait(pe, ln2_step[layer], LN_STEPS * (i - 2))
                            for c in range(KD):
                                mm = nc.tensor.transpose(ps_x2T[:, c * P:(c + 1) * P], xln2[:, (d - 3) % 2, c * P:(c + 1) * P], ident)
                        mm.then_inc(turned_mm[layer], 1)
                    if live(i, 2):
                        wait(pe, pblk_ready[layer], BLK * (i - 1))
                        wait(pe, v_ready[layer], i - 1)
                        wait(pe, oT_ready[layer], i - 2)
                        attend(0, 8, d).then_inc(o_mm[layer], 1)
                    if live(i, 3):
                        wait(pe, turned_ready[layer], i + 1)
                        wait(pe, o_ready[layer], 2 * (i - 2))
                        e = E[layer]
                        for k in range(KD):
                            mm = nc.tensor.matmul(ps_route[:, 0:e], xln2T[:, k], w_gate[:, k, 0:e], start=k == 0, stop=k == KD - 1)
                        mm.then_inc(route_mm[layer], 1)
                    if live(i, 0):
                        if isinstance(i, int) and i == 0:
                            pe.wait_ge(small_in[layer], SMALL + 16 * (1 - layer))
                        wait(pe, turned_ready[layer], i + 1)
                        wait(pe, qk_ready[layer], 4 * i)
                        for c in range(4):
                            for k in range(KD):
                                mm = nc.tensor.matmul(ps_qk[:, c * P:(c + 1) * P], w_qkv[:, k, c * P:(c + 1) * P], xlnT[:, k],
                                                      start=k == 0, stop=k == KD - 1)
                        mm.then_inc(qk_mm[layer], 1)
                    if live(i, 2):
                        wait(pe, rt_step[layer], RT_STEPS * (i - 3) + 1)
                        attend(8, 12, d)
                    if layer == 1 and live(i, 0):
                        wait(pe, rot_ready, 2 * i)
                        wait(pe, rt_step[1], RT_STEPS * (i - 4) + 12)
                        wait(pe, pblk_ready[1], BLK * (i - 1))
                        for c in range(4):
                            wait(pe, qk_ready[1], 4 * i + c + 1)
                            mm = nc.tensor.matmul(ps_swap[:, c * P:(c + 1) * P], const("swap"), qk_raw[:, c], start=True, stop=True)
                        mm.then_inc(swap_mm, 1)
                    if live(i, 2):
                        attend(12, 16, d).then_inc(o_mm[layer], 1)
                    if live(i, 1):
                        wait(pe, p_ready[layer], i)
                        wait(pe, rt_step[layer], RT_STEPS * (i - 4) + 12)
                        if layer == 1:
                            wait(pe, rot_ready, 2 * min(i + 1, NT) if isinstance(i, int) else 2 * (i + 1))
                        for c in range(2):
                            mm = nc.tensor.transpose(ps_pT[:, c * P:(c + 1) * P],
                                                     p_sb[:, c * IPT:(c + 1) * IPT].rearrange("p b k -> p (b k)"), ident)
                        mm.then_inc(pT_mm[layer], 1)
                    if live(i, 2):
                        wait(pe, o_ready[layer], 2 * (i - 1))
                        for c in range(KD):
                            mm = nc.tensor.transpose(ps_oT[:, c * P:(c + 1) * P], o_sb[:, c * P:(c + 1) * P], ident)
                        mm.then_inc(oT_mm[layer], 1)
                    if live(i, 0):
                        wait(pe, v_ready[layer], i)
                        for k in range(KD):
                            mm = nc.tensor.matmul(ps_v, xlnT[:, k], w_qkv[:, k, 2 * D:3 * D], start=k == 0, stop=k == KD - 1)
                        mm.then_inc(v_mm[layer], 1)
                    if live(i, 2):
                        wait(pe, oT_ready[layer], i - 1)
                        for k in range(KD):
                            mm = nc.tensor.matmul(ps_proj, oT[:, k], w_proj[:, k], start=k == 0, stop=k == KD - 1)
                        mm.then_inc(proj_mm[layer], 1)
                steps(pe, step)

            def moe(layer):
                n, hid = NTILE[layer], HID[layer]
                chunks = HPAD[layer] // P
                parts = 1 if layer == 0 else 2
                width = hid // parts
                at_g, at_u, at_d = (KD * hid, 0, 2 * KD * hid) if layer == 0 else (0, KD * hid, 2 * KD * hid)

                def expert_of(j):
                    return pe.value_load(tile_exp[0:1, bass.ds(j, 1)], min_val=0, max_val=E[layer] - 1)

                def turn_in(j):
                    pe.wait_ge(gather_in[layer], 16 * j + 16)
                    wait(pe, gT_ready[layer], j)
                    for c in range(KD):
                        mm = nc.tensor.transpose(ps_gT[:, c * P:(c + 1) * P], xg[:, c * P:(c + 1) * P], ident)
                    mm.then_inc(gT_mm[layer], 1)

                def into(ps, at, e, done):
                    for s in range(parts):
                        for k in range(KD):
                            mm = nc.tensor.matmul(ps[:, s, 0:width], xgT[:, k],
                                                  experts[:, bass.ds(e * SLOT + at + k * hid + s * width, width)],
                                                  start=k == 0, stop=k == KD - 1)
                    mm.then_inc(done, 1)

                def gate(j, e):
                    pe.wait_ge(gT_ready[layer], j + 1)
                    wait(pe, gbias_ready[0] if layer == 0 else silu_ready[1], j)
                    into(ps_g, at_g, e, g_mm[layer])

                def up(j, e):
                    wait(pe, act_ready[layer], j)
                    into(ps_u, at_u, e, u_mm[layer])

                def turn_act(j):
                    pe.wait_ge(act_ready[layer], j + 1)
                    wait(pe, aT_ready[layer], parts * j)
                    for c in range(chunks):
                        mm = nc.tensor.transpose(ps_aT[c // 4][:, (c % 4) * P:(c % 4 + 1) * P], act[:, c * P:(c + 1) * P], ident)
                    mm.then_inc(aT_mm[layer], 1)

                def down(j, e):
                    pe.wait_ge(aT_ready[layer], parts * (j + 1))
                    wait(pe, yb_ready[0] if layer == 0 else y_ready[1], j)
                    for k in range(chunks):
                        mm = nc.tensor.matmul(ps_y[:, 0:D], actT[:, k], experts[:, bass.ds(e * SLOT + at_d + k * D, D)],
                                              start=k == 0, stop=k == chunks - 1)
                    mm.then_inc(y_mm[layer], 1)

                pe.wait_ge(experts_in[layer], W_DMAS[layer])
                pe.wait_ge(tt_step[layer], TT_STEPS)
                if layer == 1:
                    pe.wait_ge(act_pad, 1)
                    pe.wait_ge(w_pad, 1)
                turn_in(0)
                first = expert_of(0)
                gate(0, first)
                up(0, first)
                turn_in(1)
                with pe.Fori(1, n - 1) as j:
                    e = expert_of(j)
                    gate(j, e)
                    turn_act(j - 1)
                    up(j, e)
                    turn_in(j + 1)
                    down(j - 1, expert_of(j - 1))
                last = expert_of(n - 1)
                gate(n - 1, last)
                turn_act(n - 2)
                up(n - 1, last)
                down(n - 2, expert_of(n - 2))
                turn_act(n - 1)
                down(n - 1, last)

            pe.wait_ge(consts_in, N_CONST)
            pe.wait_ge(tokw_in, 48)
            pe.wait_ge(cast_done, 3)
            pe.wait_ge(pad_done, 2)
            for layer in range(2):
                attention(layer)
                moe(layer)


def _constants(np):
    p = np.arange(P)
    c = np.zeros((P, NCONST), np.float32)

    def put(name, v):
        at, n = CONSTS[name]
        c[:, at:at + n] = np.asarray(v, np.float32).reshape(-1, n)

    put("ident", np.eye(P))
    put("swap", np.eye(P)[p ^ 1])
    put("upper", p[:, None] < p[None, :])
    put("ones", np.ones((P, P)))
    pos = np.arange(NPATCH)
    freq = (np.float32(10000.0) ** (-2.0 * np.arange(HD // 2, dtype=np.float32) / HD)).astype(np.float32)
    angle = pos.astype(np.float32)[None, :] * freq[(p % HD) // 2][:, None]
    put("cos", np.cos(angle))
    put("sin", np.sin(angle) * np.where(p % 2 == 0, -1.0, 1.0)[:, None])
    q = (p % 16)[:, None, None]
    head = np.arange(2)[None, :, None] * HPC + (p // 16)[:, None, None]
    k = pos[None, None, :]
    hidden = k > q
    put("mask0", np.where(hidden, -1e30, (k - q) * 0.5 ** (head + 1.0)).reshape(P, 32))
    put("mask1", np.where(hidden + 0 * head, -1e30, 0.0).reshape(P, 32))
    put("block", (p // 16)[:, None] == np.arange(8)[None, :])
    put("tokid", p[:, None] + P * np.arange(NT)[None, :])
    put("eoff", np.arange(9) * TOK)
    put("eidx", np.arange(9))
    put("steps", np.arange(16) * P)
    put("tri", np.arange(9)[:, None] >= np.arange(9)[None, :])
    put("tile", np.arange(JMAX))
    put("nhalf", -0.5)
    return c


def kernel(**inputs):
    import numpy as np
    import concourse.bacc as bacc
    from concourse.bass_utils import run_bass_kernel_spmd as run

    x = {name: np.asarray(v) for name, v in inputs.items()}

    def rows(w):
        return w.reshape(-1, P, w.shape[-1]).transpose(1, 0, 2)

    def experts(w):
        return w.reshape(w.shape[0], -1, P, w.shape[-1]).transpose(0, 2, 1, 3).reshape(w.shape[0], P, -1)

    patches = x["x"].reshape(IMGS, 3, 4, 16, 4, 16).transpose(1, 3, 5, 0, 2, 4)
    patches = patches.reshape(KF, P, NT, P).transpose(2, 1, 0, 3).reshape(NT * P, KF * P)
    a = {
        "consts": _constants(np),
        "zeros": np.zeros((P, D), np.float32),
        "patches": patches,
        "w_tok": rows(x["L0_tok_W"].T),
        "b_tok": x["L0_tok_b"],
        "pos": np.tile(x["L0_tok_pos_emb"], (IPT, 1)),
        "w_gate0": rows(x["L0_ffn_gate_w"].T),
        "b_gate": x["L0_ffn_gate_b"],
        "w_gate1": rows(x["L1_ffn_Wr"]),
        "w_up0": experts(x["L0_ffn_w0"].transpose(0, 2, 1)),
        "w_gate_h0": experts(x["L0_ffn_w1"].transpose(0, 2, 1)),
        "w_down0": experts(x["L0_ffn_w2"].transpose(0, 2, 1)),
        "b_exp": np.concatenate([x["L0_ffn_b0"], x["L0_ffn_b1"], x["L0_ffn_b2"]], axis=1),
        "w_gate_h1": experts(x["L1_ffn_Wg"]),
        "w_up1": experts(x["L1_ffn_Wu"]),
        "w_down1": x["L1_ffn_Wd"],
    }
    for layer, w, b in ((0, "L0_attn_W_attn", "L0_attn_b_attn"), (1, "L1_attn_W_qkv", "L1_attn_b_qkv")):
        a[f"w_qkv{layer}"] = rows(x[w])
        a[f"b_qk{layer}"] = x[b][:2 * D].reshape(4, P).T
        a[f"b_v{layer}"] = x[b][2 * D:]
        a[f"w_proj{layer}"] = rows(x[f"L{layer}_attn_W_proj"])
        a[f"b_proj{layer}"] = x[f"L{layer}_attn_b_proj"]
    for layer in range(2):
        empty = np.zeros(((E[layer] + 1) * TOK, 2), np.int32)
        empty[:, 0] = DUMMY + np.arange(len(empty)) % P
        a[f"empty{layer}"] = empty

    nc = bacc.Bacc("TRN2", target_bir_lowering=False, num_devices=1)
    arrays, aps = {}, {}
    for name, v in a.items():
        v = np.ascontiguousarray(v)
        arrays[f"in_{name}"] = v
        aps[name] = nc.dram_tensor(f"in_{name}", v.shape, mybir.dt.from_np(v.dtype), kind="ExternalInput").ap()
    tables = {
        "resid": nc.dram_tensor("resid", (ROWS, D), F32, kind="Internal").ap(),
        "normed0": nc.dram_tensor("normed0", (ROWS, D), F32, kind="Internal").ap(),
        "normed1": nc.dram_tensor("normed1", (ROWS, D), F32, kind="Internal").ap(),
        "table0": nc.dram_tensor("table0", ((E[0] + 1) * TOK, 2), I32, kind="Internal").ap(),
        "table1": nc.dram_tensor("table1", ((E[1] + 1) * TOK, 2), I32, kind="Internal").ap(),
    }
    out = nc.dram_tensor("out_0", (ROWS, D), F32, kind="ExternalOutput").ap()
    tower(nc, aps, tables, out)
    r = run(nc, [arrays], core_ids=[0])
    return r.results[0]["out_0"][:TOK].reshape(IMGS, NPATCH, D)
```

```python
from contextlib import ExitStack

import concourse.bass as bass
from concourse import mybir

F32 = mybir.dt.float32
BF16 = mybir.dt.bfloat16
I32 = mybir.dt.int32
U32 = mybir.dt.uint32
ALU = mybir.AluOpType
ACT = mybir.ActivationFunctionType
AX = mybir.AxisListType

P = 128
D = 256
KD = D // P
IMGS, NPATCH = 128, 16
TOK = IMGS * NPATCH
NT = TOK // P
IPT = P // NPATCH
NH, HD = 16, 16
HPC = P // HD
FEAT = 768
KF = FEAT // P
PAD = 48
WIN = HD + PAD
EPS = 1e-5
UNROLL = 4
LAG_RANK = 4

E = (8, 9)
HID = (512, 704)
HPAD = (512, 768)
NTILE = tuple(TOK * 2 // P + e - 1 for e in E)
JMAX = max(NTILE)
SLOT = 4352
DUMMY = TOK
ROWS = TOK + P

CONSTS = {}


def _columns():
    at = 0
    for name, n in (("ident", P), ("swap", P), ("upper", P), ("ones", P), ("cos", 16), ("sin", 16),
                    ("mask0", 32), ("mask1", 32), ("block", 8), ("tokid", NT), ("eoff", 9),
                    ("eidx", 9), ("steps", 16), ("tri", 81), ("tile", JMAX), ("nhalf", 1)):
        CONSTS[name] = (at, n)
        at += n
    return at


NCONST = _columns()


def tower(nc, a, tables, out):
    with ExitStack() as ctx:
        def sb(name, shape, dt=F32):
            return ctx.enter_context(nc.sbuf_tensor(name, shape, dt))

        def sem(name):
            return ctx.enter_context(nc.semaphore(name))

        def sem2(name):
            return [sem(f"{name}_{layer}") for layer in range(2)]

        experts = sb("experts", [P, 9 * SLOT])
        consts = sb("consts", [P, NCONST])
        w_qkv = sb("w_qkv", [P, KD, 3 * D])
        w_proj = sb("w_proj", [P, KD, D])
        bias_qk = sb("bias_qk", [P, 4])
        bias_v = sb("bias_v", [P, D])
        bias_proj = sb("bias_proj", [P, D])
        w_gate = sb("w_gate", [P, KD, 9])
        bias_gate = sb("bias_gate", [P, 8])
        h = sb("h", [P, UNROLL, D])
        xln = sb("xln", [P, D])
        turned = sb("turned", [P, 2, KD, P])
        xlnT, xln2T = turned[:, 0], turned[:, 1]
        qk_raw = sb("qk_raw", [P, 4, P])
        rot = sb("rot", [P, 4, P])
        q_sb = sb("q_sb", [P, KD, P])
        k_sb = sb("k_sb", [P, KD, P + PAD])
        v_sb = sb("v_sb", [P, 2, D + PAD])
        spread = sb("spread", [P, 2 * 2 * IPT * P])
        qblk = spread[:, 0:2048].rearrange("p (u g n) -> p u g n", g=HPC, n=16)
        pblk = spread[:, 2048:4096].rearrange("p (g b n) -> p g b n", b=IPT, n=16)
        s_sb = sb("s_sb", [P, 2 * IPT, 16])
        p_sb = sb("p_sb", [P, 2 * IPT, 16])
        s_max = sb("s_max", [P, 2 * IPT])
        s_sum = sb("s_sum", [P, 2 * IPT])
        s_inv = sb("s_inv", [P, 2 * IPT])
        o_sb = sb("o_sb", [P, D])
        oT = sb("oT", [P, KD, P])
        xln2 = sb("xln2", [P, 2, D])
        stats = sb("stats", [P, 2, 6])
        moments = sb("moments", [P, 2, 2])
        var_eps = sb("var_eps", [P, 2])
        rstd = sb("rstd", [P, 2])
        upper_bf = sb("upper_bf", [P, P], BF16)
        ones_bf = sb("ones_bf", [P, P], BF16)
        tok_id = sb("tok_id", [P, NT], I32)
        logits = sb("logits", [P, 9])
        top = sb("top", [P, 8])
        top_i = sb("top_i", [P, 8], U32)
        top_f = sb("top_f", [P, 2])
        gap = sb("gap", [P, 1])
        egap = sb("egap", [P, 1])
        wgt = sb("wgt", [P, 2])
        pick = sb("pick", [P, 2, 9])
        both_bf = sb("both_bf", [P, 9], BF16)
        place = sb("place", [P, 9])
        prod = sb("prod", [P, 9])
        count = sb("count", [P, 9])
        table_in = sb("table_in", [P, 1])
        slot_f = sb("slot_f", [P, 2])
        slot_i = sb("slot_i", [P, UNROLL, 2], I32)
        entry = sb("entry", [P, UNROLL, 2, 2], I32)
        tt_n = spread[0:1, 1024:1168].rearrange("p (e i) -> p e i", i=16)
        tt_tiles = spread[0:1, 1168:1177]
        tt_tri = spread[0:1, 1184:1265].rearrange("p (x y) -> p x y", y=9)
        tt_end = spread[0:1, 1280:1289]
        tt_ge = spread[0:1, 0:9 * JMAX].rearrange("p (j e) -> p j e", e=9)
        tt_gt = spread[0:1, 9 * JMAX:18 * JMAX].rearrange("p (j e) -> p j e", e=9)
        tt_e, tt_s, tt_r, tt_r2 = (spread[0:1, at:at + JMAX] for at in (1296, 1344, 1392, 1440))
        tile_row = sb("tile_row", [1, JMAX], I32)
        tile_exp = sb("tile_exp", [1, JMAX], I32)
        places = sb("places", [P, JMAX, 2], I32)
        idx_g = sb("idx_g", [P, 1], I32)
        idx_s = sb("idx_s", [P, 1], I32)
        gate_in = spread[:, 0:512]
        gated = spread[:, 512:1216]
        up_in = spread[:, 1216:1728]
        act = spread[:, 1728:2496]
        actT = spread[:, 2496:3264].rearrange("p (c n) -> p c n", n=P)

        xg = spread[:, 3264:3520]
        xgT = spread[:, 3520:3776].rearrange("p (c n) -> p c n", c=KD)
        y_sb = spread[:, 3776:4032]

        def const(name):
            at, n = CONSTS[name]
            return consts[:, at:at + n]

        tail = experts[:, 8 * SLOT:9 * SLOT]
        w_tok = tail[:, 0:KF * D].rearrange("p (k n) -> p k n", k=KF)
        patch = tail[:, KF * D:KF * D + 2 * FEAT].rearrange("p (s k n) -> p s k n", s=2, k=KF)
        pos = tail[:, KF * D + 2 * FEAT:KF * D + 2 * FEAT + D]
        bias_tok = tail[:, KF * D + 2 * FEAT + D:KF * D + 2 * FEAT + 2 * D]
        by_expert = experts[:, :].rearrange("p (e n) -> p e n", n=SLOT)

        bank = [ctx.enter_context(nc.psum_tensor(f"bank{i}", [P, 512], F32)) for i in range(4)]
        pair45 = ctx.enter_context(nc.psum_tensor("bank45", [P, 2, 512], F32))
        pair67 = ctx.enter_context(nc.psum_tensor("bank67", [P, 2, 512], F32))
        ps_tok, ps_v = bank[0][:, 0:D], bank[0][:, D:2 * D]
        ps_xT, ps_x2T = bank[1][:, 0:D], bank[1][:, D:2 * D]
        ps_qk, ps_swap = bank[2], bank[3]
        ps_sc = pair45[:, :, :]
        ps_pT, ps_proj = bank[3][:, D:2 * D], pair45[:, 1, 0:D]
        ps_o = pair67[:, :, :]
        ps_oT, ps_rank = pair67[:, 0, 0:D], bank[3][:, 0:32]

        def ps_route(t):
            return ps_qk[:, 0:9] if isinstance(t, int) and t >= NT - 3 else pair67[:, 1, 0:9]

        ps_g, ps_u = pair45, pair67
        ps_aT = [bank[0], bank[1]]
        ps_y, ps_gT = bank[2], bank[3]

        consts_in = sem("consts_in")
        small_in = sem2("small_in")
        tokw_in, pos_in = sem("tokw_in"), sem("pos_in")
        cast_done = sem("cast_done")
        pad_done = sem("pad_done")
        pos_done = sem("pos_done")
        patch_in = [sem("patch_in_even"), sem("patch_in_odd")]
        h_in = [sem(f"h_in_{s}") for s in range(UNROLL)]
        experts_in = sem2("experts_in")
        dummies_in = sem("dummies_in")
        tok_mm = sem("tok_mm")
        h_ready = sem2("h_ready")
        hb_ready = sem2("hb_ready")
        ln_step = sem2("ln_step")
        rstd_ready, rstd2_ready = sem2("rstd_ready"), sem2("rstd2_ready")
        turned_mm, turned_ready = sem2("turned_mm"), sem2("turned_ready")
        qk_mm, qk_ready = sem2("qk_mm"), sem2("qk_ready")
        swap_mm, cos_ready, rot_ready = sem("swap_mm"), sem("cos_ready"), sem("rot_ready")
        rope_done = sem("rope_done")
        qblk_ready = sem2("qblk_ready")
        v_mm, v_ready = sem2("v_mm"), sem2("v_ready")
        sc_mm, sm_step, exp_ready, p_ready = sem2("sc_mm"), sem2("sm_step"), sem2("exp_ready"), sem2("p_ready")
        pT_mm, pblk_ready = sem2("pT_mm"), sem2("pblk_ready")
        o_mm, o_ready = sem2("o_mm"), sem2("o_ready")
        oT_mm, oT_ready = sem2("oT_mm"), sem2("oT_ready")
        proj_mm, h2_ready = sem2("proj_mm"), sem2("h2_ready")
        ln2_step = sem2("ln2_step")
        h2_out = [[sem(f"h2_out_{layer}_{s}") for s in range(UNROLL)] for layer in range(2)]
        xln2_out = [[sem(f"xln2_out_{layer}_{s}") for s in range(2)] for layer in range(2)]
        route_mm, rt_step, egap_ready = sem2("route_mm"), sem2("rt_step"), sem2("egap_ready")
        rank_mm, entry_ready, entry_out = sem2("rank_mm"), sem2("entry_ready"), sem2("entry_out")
        slot_step, wgt_in = sem2("slot_step"), sem2("wgt_in")
        tt_step, tt_sum = sem2("tt_step"), sem2("tt_sum")
        count_zero, act_pad, w_pad = sem("count_zero"), sem("act_pad"), sem("w_pad")
        waited, table_used = sem("waited"), sem("table_used")
        places_in = [[sem(f"places_in_{layer}_{s}") for s in range(UNROLL)] for layer in range(2)]
        idx_g_ready, gather_in = sem2("idx_g_ready"), sem2("gather_in")
        gT_mm, gT_ready = sem2("gT_mm"), sem2("gT_ready")
        g_mm, u_mm = sem2("g_mm"), sem2("u_mm")
        gbias_ready, ubias_ready, silu_ready, act_ready = sem2("gbias_ready"), sem2("ubias_ready"), sem2("silu_ready"), sem2("act_ready")
        aT_mm, aT_ready = sem2("aT_mm"), sem2("aT_ready")
        y_mm, yb_ready, y_ready = sem2("y_mm"), sem2("yb_ready"), sem2("y_ready")
        idx_s_ready, added = sem2("idx_s_ready"), sem2("added")

        N_CONST = 16
        SMALL = 6 * 16
        LN_STEPS = 4
        SM_STEPS = 6
        RT_STEPS = 14
        BLK = HPC
        ACT_BLK = (0, 2)
        TT_STEPS = 11
        W_DMAS = (4 * E[0] * 16, 4 * E[1] * 16)
        RESID = [tables["resid"], out]
        NORMED = [tables["normed0"], tables["normed1"]]
        TABLE = [tables["table0"], tables["table1"]]

        def steps(engine, step):
            total = NT + LAG_RANK
            for i in range(UNROLL):
                step(i, i)
            with engine.Fori(1, NT // UNROLL) as group:
                for d in range(UNROLL):
                    step(group * UNROLL + d, d)
            for i in range(NT, total):
                step(i, i % UNROLL)

        def turns(engine, n, step):
            for j in range(UNROLL):
                step(j, j)
            with engine.Fori(1, n // UNROLL) as group:
                for s in range(UNROLL):
                    step(group * UNROLL + s, s)
            for j in range(n // UNROLL * UNROLL, n):
                step(j, j % UNROLL)

        def live(i, lag):
            return not isinstance(i, int) or 0 <= i - lag < NT

        def wait_turn(engine, semaphores, i, d, lag):
            n = len(semaphores)
            at = d - lag
            if live(i, lag):
                if isinstance(i, int):
                    engine.wait_ge(semaphores[at % n], 16 * ((i - lag) // n + 1))
                else:
                    engine.wait_ge(semaphores[at % n], (i - d) * (16 // n) + 16 * (at // n + 1))

        def wait(engine, semaphore, value):
            if not isinstance(value, int) or value > 0:
                engine.wait_ge(semaphore, value)

        def apart(engine):
            engine.sem_inc(waited, 1)

        def in_heads(x, part):
            return x[:, 2 * part:2 * part + 2].rearrange("p c (b n) -> p (c b) n", n=NPATCH)

        def rotary(name):
            return const(name).unsqueeze(1).to_broadcast([P, KD * IPT, NPATCH])

        def expert_registers(engine, layer):
            held, last = engine.alloc_register(f"expert_{layer}"), engine.alloc_register(f"expert_before_{layer}")
            top = E[layer] - 1

            def now():
                return engine.snap(held, min_val=0, max_val=top)

            def before():
                return engine.snap(last, min_val=0, max_val=top)

            def load(j):
                engine.reg_mov(last, held)
                engine.reg_load(held, tile_exp[0:1, bass.ds(j, 1)])

            engine.reg_load(held, tile_exp[0:1, 0:1])
            return load, now, before

        block = ctx.enter_context(nc.Block())

        @block.sync
        def _(sp):
            sp.dma_start(consts[:], a["consts"]).then_inc(consts_in, N_CONST)
            sp.dma_start(w_tok, a["w_tok"]).then_inc(tokw_in, 16)

            def small(layer):
                sp.dma_start(w_qkv[:], a[f"w_qkv{layer}"]).then_inc(small_in[layer], 16)
                sp.dma_start(bias_qk[:], a[f"b_qk{layer}"]).then_inc(small_in[layer], 16)
                sp.dma_start(bias_v[:], a[f"b_v{layer}"].partition_broadcast(P)).then_inc(small_in[layer], 16)
                sp.dma_start(bias_proj[:], a[f"b_proj{layer}"].partition_broadcast(P)).then_inc(small_in[layer], 16)
                sp.dma_start(w_proj[:], a[f"w_proj{layer}"]).then_inc(small_in[layer], 16)
                sp.dma_start(w_gate[:, :, 0:E[layer]], a[f"w_gate{layer}"]).then_inc(small_in[layer], 16)
                if layer == 0:
                    sp.dma_start(bias_gate[:], a["b_gate"].partition_broadcast(P)).then_inc(small_in[0], 16)

            def attention(layer):
                def step(i, d):
                    if layer == 0 and live(i, 0):
                        wait(sp, tok_mm, i - 1)
                        sp.dma_start(patch[:, d % 2], a["patches"][bass.ts(i, P), :].rearrange("p (k n) -> p k n", k=KF)).then_inc(patch_in[d % 2], 16)
                        if isinstance(i, int) and i == 0:
                            sp.dma_start(pos, a["pos"]).then_inc(pos_in, 16)
                            sp.dma_start(bias_tok, a["b_tok"].partition_broadcast(P)).then_inc(pos_in, 16)
                            small(0)
                        if isinstance(i, int) and i == 1:
                            for table, n in ((0, E[0]), (1, E[1])):
                                sp.dma_start(TABLE[table], a[f"empty{table}"]).then_inc(dummies_in, 16)
                            for rows in (RESID[0], NORMED[0], NORMED[1], RESID[1]):
                                sp.dma_start(rows[DUMMY:ROWS, :], a["zeros"]).then_inc(dummies_in, 16)
                    if layer == 1 and live(i, 0):
                        wait_turn(sp, h2_out[1], i, d, 4)
                        apart(sp)
                        wait(sp, ln2_step[1], LN_STEPS * (i - 3))
                        sp.dma_start(h[:, d], RESID[0][bass.ts(i, P), :]).then_inc(h_in[d], 16)
                    if live(i, 3):
                        wait(sp, h2_ready[layer], i - 2)
                        sp.dma_start(RESID[layer][bass.ts(i - 3, P), :], h[:, (d - 3) % UNROLL]).then_inc(h2_out[layer][(d - 3) % UNROLL], 16)
                        wait(sp, ln2_step[layer], LN_STEPS * (i - 2))
                        sp.dma_start(NORMED[layer][bass.ts(i - 3, P), :], xln2[:, (d - 3) % 2]).then_inc(xln2_out[layer][(d - 3) % 2], 16)
                steps(sp, step)

            def moe(layer):
                sp.wait_ge(tt_step[layer], TT_STEPS)
                sp.wait_ge(entry_out[layer], 32 * NT)
                if layer == 1:
                    sp.wait_ge(idx_s_ready[0], NTILE[0])
                    sp.wait_ge(y_ready[0], NTILE[0])

                def load(j, s):
                    wait(sp, places_in[layer][s], 16 * (j // UNROLL) if isinstance(j, int) else (j - s) * (16 // UNROLL))
                    if not isinstance(j, int):
                        apart(sp)
                    row = sp.value_load(tile_row[0:1, bass.ds(j, 1)], min_val=0, max_val=(E[layer] + 1) * TOK - P)
                    sp.dma_start(places[:, bass.ds(j, 1), :], TABLE[layer][bass.ds(row, P), :].rearrange("p (o n) -> p o n", o=1)).then_inc(places_in[layer][s], 16)

                turns(sp, NTILE[layer], load)

            attention(0)
            moe(0)
            for used, times in ((qk_ready, 4), (v_ready, 1), (hb_ready, 1), (proj_mm, 1), (route_mm, 1)):
                sp.wait_ge(used[0], times * NT)
            small(1)
            sp.wait_ge(added[0], 16 * NTILE[0])
            attention(1)
            moe(1)
            for stored in h2_out[1]:
                sp.wait_ge(stored, 16 * NT // UNROLL)
            sp.wait_ge(dummies_in, 6 * 16)
            sp.wait_ge(added[1], 16 * NTILE[1])

        @block.gpsimd
        def _(pool):
            nc.gpsimd.memset(k_sb[:, :, P:P + PAD], 0.0).then_inc(pad_done, 1)
            nc.gpsimd.memset(v_sb[:, :, D:D + PAD], 0.0).then_inc(pad_done, 1)
            pool.wait_ge(consts_in, N_CONST)
            nc.gpsimd.tensor_copy(upper_bf[:], const("upper")).then_inc(cast_done, 1)
            nc.gpsimd.tensor_copy(ones_bf[:], const("ones")).then_inc(cast_done, 1)
            nc.gpsimd.tensor_copy(tok_id[:], const("tokid")).then_inc(cast_done, 1)
            pool.wait_ge(pos_in, 32)
            nc.gpsimd.tensor_tensor(pos, pos, bias_tok, ALU.add).then_inc(pos_done, 1)

            def attention(layer):
                def step(i, d):
                    if live(i, 3):
                        wait(pool, ln2_step[layer], LN_STEPS * (i - 3) + 3)
                        nc.gpsimd.tensor_tensor(rstd[:, 1:2], var_eps[:, 1:2], const("nhalf"), ALU.pow).then_inc(rstd2_ready[layer], 1)
                    if live(i, 0):
                        wait(pool, ln_step[layer], LN_STEPS * i + 3)
                        nc.gpsimd.tensor_tensor(rstd[:, 0:1], var_eps[:, 0:1], const("nhalf"), ALU.pow).then_inc(rstd_ready[layer], 1)
                        if isinstance(i, int) and i == 0:
                            pool.wait_ge(small_in[layer], SMALL + 16 * (1 - layer))
                        wait(pool, ln_step[layer], LN_STEPS * (i + 1))
                        nc.gpsimd.tensor_tensor(h[:, d], h[:, d], bias_proj[:], ALU.add).then_inc(hb_ready[layer], 1)
                    if live(i, 4):
                        if layer == 0 and isinstance(i, int) and i == 4:
                            pool.wait_ge(dummies_in, 6 * 16)
                        wait(pool, entry_ready[layer], i - 3)
                        for c in range(2):
                            apart(pool)
                            nc.gpsimd.indirect_dma_start(
                                out=TABLE[layer], out_offset=bass.IndirectOffsetOnAxis(slot_i[:, d, c:c + 1], 0),
                                in_=entry[:, d, c], in_offset=None).then_inc(entry_out[layer], 16)
                    if layer == 1 and live(i, 0):
                        for part in range(2):
                            wait(pool, qk_ready[1], 4 * i + 2 * part + 2)
                            nc.gpsimd.tensor_tensor(in_heads(rot, part), in_heads(qk_raw, part), rotary("cos"), ALU.mult).then_inc(cos_ready, 1)
                    if live(i, 4):
                        wait(pool, entry_out[layer], 32 * (i - 3))
                steps(pool, step)

            def moe(layer):
                n = NTILE[layer]
                for stored in xln2_out[layer] + h2_out[layer]:
                    pool.wait_ge(stored, 16 * NT // (2 if stored in xln2_out[layer] else UNROLL))

                def gather(j, s):
                    pool.wait_ge(places_in[layer][s], 16 * (j // UNROLL + 1) if isinstance(j, int) else (j - s) * (16 // UNROLL) + 16)
                    wait(pool, gather_in[layer], 16 * j)
                    if not isinstance(j, int):
                        apart(pool)
                    nc.gpsimd.tensor_copy(idx_g[:], places[:, bass.ds(j, 1), 0]).then_inc(idx_g_ready[layer], 1)
                    wait(pool, gT_mm[layer], j)
                    pool.wait_ge(idx_g_ready[layer], j + 1)
                    apart(pool)
                    nc.gpsimd.indirect_dma_start(out=xg, out_offset=None, in_=NORMED[layer],
                                                 in_offset=bass.IndirectOffsetOnAxis(idx_g[:, 0:1], 0)).then_inc(gather_in[layer], 16)

                def add(j):
                    wait(pool, added[layer], 16 * j)
                    if not isinstance(j, int):
                        apart(pool)
                    nc.gpsimd.tensor_copy(idx_s[:], places[:, bass.ds(j, 1), 0]).then_inc(idx_s_ready[layer], 1)
                    pool.wait_ge(y_ready[layer], j + 1)
                    pool.wait_ge(idx_s_ready[layer], j + 1)
                    apart(pool)
                    nc.gpsimd.indirect_dma_start(out=RESID[layer], out_offset=bass.IndirectOffsetOnAxis(idx_s[:, 0:1], 0),
                                                 in_=y_sb, in_offset=None, compute_op=ALU.add).then_inc(added[layer], 16)

                def both(j, s):
                    gather(j, s)
                    if not isinstance(j, int) or j >= 3:
                        add(j - 3)

                turns(pool, n, both)
                for j in range(n - 3, n):
                    add(j)

            for layer in range(2):
                if layer == 1:
                    pool.wait_ge(y_mm[0], NTILE[0])
                    nc.gpsimd.memset(by_expert[64:P, :, SLOT - D:SLOT], 0.0).then_inc(w_pad, 1)
                    pool.wait_ge(w_pad, 1)
                attention(layer)
                moe(layer)

        @block.scalar
        def _(act_e):
            def load_expert(layer, times):
                def load(at, n, rows, source):
                    to = experts[rows, bass.ds(times(SLOT) + at, n)]
                    if len(source.shape) > 2:
                        to = to.rearrange("p (k n) -> p k n", n=D)
                    act_e.dma_start(to, source).then_inc(experts_in[layer], 16)

                every = slice(0, P)
                if layer == 0:
                    for at, name in ((0, "w_up0"), (1024, "w_gate_h0"), (2048, "w_down0")):
                        load(at, 1024, every, a[name][bass.ds(times(P), P), :])
                    load(3072, 1280, every, a["b_exp"][bass.ds(times(1280), 1280)].partition_broadcast(P))
                else:
                    for at, name in ((0, "w_gate_h1"), (1408, "w_up1")):
                        load(at, 1408, every, a[name][bass.ds(times(P), P), :])
                    load(2816, 1280, every, a["w_down1"][bass.ds(times(HID[1]), 640), :].rearrange("(k p) n -> p k n", p=P))
                    load(4096, 256, slice(0, 64), a["w_down1"][bass.ds(times(HID[1]) + 640, 64), :])

            def attention(layer):
                def take_heads(t, s):
                    wait(act_e, o_mm[layer], 2 * t + s + 1)
                    nc.scalar.activation(o_sb[:, s * P:(s + 1) * P].rearrange("p (g n) -> p g n", n=HD),
                                         ps_o[:, s].rearrange("p (g w) -> p g w", w=WIN)[:, :, 0:HD], ACT.Copy).then_inc(o_ready[layer], 1)

                def gap_exponential(i):
                    wait(act_e, rt_step[layer], RT_STEPS * (i - 3) + 4)
                    nc.scalar.activation(egap[:], gap[:], ACT.Exp).then_inc(egap_ready[layer], 1)

                def step(i, d):
                    last = isinstance(i, int) and NT <= i <= NT + 1
                    if live(i, 0) or live(i, 3):
                        wait(act_e, turned_mm[layer], i + 1)
                        if live(i, 0):
                            wait(act_e, v_mm[layer], i)
                        if live(i, 3):
                            wait(act_e, route_mm[layer], i - 3)
                        lo, hi = 0 if live(i, 0) else 1, 2 if live(i, 3) else 1
                        nc.scalar.activation(turned[:, lo:hi].rearrange("p s c n -> p (s c n)"), bank[1][:, lo * D:hi * D], ACT.Copy).then_inc(turned_ready[layer], 1)
                    if live(i, 1):
                        wait(act_e, sm_step[layer], SM_STEPS * (i - 1) + 4)
                        nc.scalar.activation(s_sb[:], s_sb[:], ACT.Exp).then_inc(exp_ready[layer], 1)
                    if live(i, 2):
                        wait(act_e, oT_mm[layer], i - 2)
                        take_heads(i - 2, 0)
                    if live(i, 0):
                        if layer == 0:
                            wait(act_e, qblk_ready[0], BLK * i)
                            wait(act_e, sc_mm[0], 2 * i)
                        else:
                            wait(act_e, rope_done, 2 * i)
                        if isinstance(i, int) and i == 0:
                            act_e.wait_ge(small_in[layer], SMALL + 16 * (1 - layer))
                            act_e.wait_ge(pad_done, 2)
                        wait(act_e, qk_mm[layer], i + 1)
                        for c in range(4):
                            to = qk_raw[:, c] if layer else (q_sb[:, c] if c < 2 else k_sb[:, c - 2, 0:P])
                            nc.scalar.activation(to, ps_qk[:, c * P:(c + 1) * P], ACT.Identity, bias=bias_qk[:, c:c + 1]).then_inc(qk_ready[layer], 1)
                    if live(i, 3) and not last:
                        gap_exponential(i)
                    if live(i, 2):
                        take_heads(i - 2, 1)
                    if live(i, 0) and ACT_BLK[layer]:
                        wait(act_e, rope_done, 2 * i + 1)
                        wait(act_e, sc_mm[layer], 2 * i)
                        for g in range(ACT_BLK[layer]):
                            nc.scalar.activation(qblk[:, :, g], q_sb[:].rearrange("p c (b n) -> p (c b) n", n=16), ACT.Copy, scale=const("block")[:, g:g + 1]).then_inc(qblk_ready[layer], 1)
                    if live(i, 2):
                        wait(act_e, oT_mm[layer], i - 1)
                        wait(act_e, proj_mm[layer], i - 2)
                        nc.scalar.activation(oT[:].rearrange("p c n -> p (c n)"), ps_oT, ACT.Copy).then_inc(oT_ready[layer], 1)
                    if last:
                        gap_exponential(i)
                    if live(i, 1):
                        wait(act_e, pT_mm[layer], i)
                        wait(act_e, o_mm[layer], 2 * (i - 1))
                        for b in range(IPT):
                            nc.scalar.activation(pblk[:, :, b], ps_pT.rearrange("p (g n) -> p g n", n=16), ACT.Copy, scale=const("block")[:, b:b + 1]).then_inc(pblk_ready[layer], 1)
                def step_and_load(i, d):
                    step(i, d)
                    peeled = E[layer] - 2 * (NT // UNROLL - 1)
                    if isinstance(i, int):
                        if 1 <= i <= peeled:
                            load_expert(layer, lambda n: (i - 1) * n)
                    elif d % 2 == 0:
                        load_expert(layer, lambda n: (i - d) * (n // 2) + (peeled - 2 + d // 2) * n)
                nc.scalar.activation(table_in[:], const("nhalf"), ACT.Exp).then_inc(table_used, 1)
                steps(act_e, step_and_load)

            def moe(layer):
                n = NTILE[layer]
                hid = HID[layer]
                gv = gated[:, 0:hid] if layer == 0 else gated[:, 0:hid].rearrange("p (s n) -> p s n", s=2)

                def gate(j):
                    wait(act_e, act_ready[layer], j)
                    if layer == 0:
                        act_e.wait_ge(gbias_ready[0], j + 1)
                        nc.scalar.activation(gv, gate_in, ACT.Silu).then_inc(silu_ready[0], 1)
                    else:
                        act_e.wait_ge(g_mm[1], j + 1)
                        nc.scalar.activation(gv, ps_g[:, :, 0:hid // 2], ACT.Silu).then_inc(silu_ready[1], 1)

                def turned_in(j):
                    act_e.wait_ge(gT_mm[layer], j + 1)
                    nc.scalar.activation(xgT.rearrange("p c n -> p (c n)"), ps_gT[:, 0:D], ACT.Copy).then_inc(gT_ready[layer], 1)

                def turned(j):
                    act_e.wait_ge(aT_mm[layer], j + 1)
                    half = actT.rearrange("p c n -> p (c n)")
                    nc.scalar.activation(half[:, 0:512], ps_aT[0][:, 0:512], ACT.Copy).then_inc(aT_ready[layer], 1)
                    if layer == 1:
                        nc.scalar.activation(half[:, 512:768], ps_aT[1][:, 0:256], ACT.Copy).then_inc(aT_ready[1], 1)

                act_e.wait_ge(egap_ready[layer], NT)
                nc.scalar.activation(table_in[:], const("nhalf"), ACT.Silu).then_inc(table_used, 1)
                turned_in(0)
                gate(0)
                turned_in(1)
                with act_e.Fori(1, n - 1) as j:
                    gate(j)
                    turned(j - 1)
                    turned_in(j + 1)
                gate(n - 1)
                turned(n - 2)
                turned(n - 1)

            act_e.wait_ge(consts_in, N_CONST)
            attention(0)
            moe(0)
            act_e.wait_ge(y_mm[0], NTILE[0])
            act_e.wait_ge(yb_ready[0], NTILE[0])
            attention(1)
            moe(1)

        @block.vector
        def _(dve):
            def layer_norms(*norms):
                for x, to, slot, done, inverse, i in norms:
                    nc.vector.bn_stats(stats[:, slot], x).then_inc(done, 1)
                for x, to, slot, done, inverse, i in norms:
                    dve.wait_ge(done, LN_STEPS * i + 1)
                    apart(dve)
                    nc.vector.bn_aggr(moments[:, slot], stats[:, slot]).then_inc(done, 1)
                for x, to, slot, done, inverse, i in norms:
                    dve.wait_ge(done, LN_STEPS * i + 2)
                    nc.vector.tensor_scalar(var_eps[:, slot:slot + 1], moments[:, slot, 1:2], EPS, None, ALU.add).then_inc(done, 1)
                for x, to, slot, done, inverse, i in norms:
                    dve.wait_ge(inverse, i + 1)
                    nc.vector.tensor_scalar(to, x, moments[:, slot, 0:1], rstd[:, slot:slot + 1], ALU.subtract, ALU.mult).then_inc(done, 1)

            def softmax(layer, t, meanwhile):
                s = SM_STEPS * t
                step_sem = sm_step[layer]
                mask = const(f"mask{layer}").rearrange("p (c k) -> p c k", c=2)
                for c in range(2):
                    dve.wait_ge(sc_mm[layer], 2 * t + c + 1)
                    nc.vector.scalar_tensor_tensor(
                        s_sb[:, c * IPT:(c + 1) * IPT], ps_sc[:, c].rearrange("p (b w) -> p b w", w=WIN)[:, :, 0:16], float(HD) ** -0.5,
                        mask[:, c:c + 1, :].to_broadcast([P, IPT, 16]), ALU.mult, ALU.add).then_inc(step_sem, 1)
                dve.wait_ge(step_sem, s + 2)
                nc.vector.tensor_reduce(s_max[:], s_sb[:], AX.X, ALU.max).then_inc(step_sem, 1)
                dve.wait_ge(step_sem, s + 3)
                nc.vector.tensor_tensor(s_sb[:], s_sb[:], s_max[:].unsqueeze(2).to_broadcast([P, 16, 16]), ALU.subtract).then_inc(step_sem, 1)
                meanwhile()
                dve.wait_ge(exp_ready[layer], t + 1)
                nc.vector.tensor_reduce(s_sum[:], s_sb[:], AX.X, ALU.add).then_inc(step_sem, 1)
                dve.wait_ge(step_sem, s + 5)
                nc.vector.reciprocal(s_inv[:], s_sum[:]).then_inc(step_sem, 1)
                dve.wait_ge(step_sem, s + 6)
                wait(dve, pT_mm[layer], t)
                nc.vector.tensor_tensor(p_sb[:], s_sb[:], s_inv[:].unsqueeze(2).to_broadcast([P, 16, 16]), ALU.mult).then_inc(p_ready[layer], 1)

            def route(layer, t):
                e = E[layer]
                s = RT_STEPS * t
                st = rt_step[layer]
                dve.wait_ge(route_mm[layer], t + 1)
                if layer == 0:
                    nc.vector.tensor_tensor(logits[:, 0:e], ps_route(t)[:, 0:e], bias_gate[:], ALU.add).then_inc(st, 1)
                else:
                    nc.vector.tensor_copy(logits[:, 0:e], ps_route(t)[:, 0:e]).then_inc(st, 1)
                dve.wait_ge(st, s + 1)
                apart(dve)
                nc.vector.max(top[:], logits[:, 0:e]).then_inc(st, 1)
                dve.wait_ge(st, s + 2)
                apart(dve)
                nc.vector.max_index(top_i[:], top[:], logits[:, 0:e]).then_inc(st, 1)
                nc.vector.tensor_tensor(gap[:], top[:, 1:2], top[:, 0:1], ALU.subtract).then_inc(st, 1)
                dve.wait_ge(st, s + 4)
                nc.vector.tensor_copy(top_f[:], top_i[:, 0:2]).then_inc(st, 1)
                dve.wait_ge(st, s + 5)
                for c in range(2):
                    nc.vector.tensor_scalar(pick[:, c, 0:e], const("eidx")[:, 0:e], top_f[:, c:c + 1], None, ALU.is_equal).then_inc(st, 1)
                dve.wait_ge(st, s + 7)
                nc.vector.tensor_tensor(both_bf[:, 0:e], pick[:, 0, 0:e], pick[:, 1, 0:e], ALU.add).then_inc(st, 1)

            def entries(layer, t, slot):
                e = E[layer]
                s = RT_STEPS * t
                st = rt_step[layer]
                dve.wait_ge(egap_ready[layer], t + 1)
                nc.vector.tensor_scalar(wgt[:, 1:2], egap[:], 1.0, None, ALU.add).then_inc(st, 1)
                dve.wait_ge(rank_mm[layer], t + 1)
                nc.vector.tensor_tensor(place[:, 0:e], ps_rank[:, 0:e], count[:, 0:e], ALU.add).then_inc(st, 1)
                dve.wait_ge(st, s + 9)
                nc.vector.reciprocal(wgt[:, 0:1], wgt[:, 1:2]).then_inc(st, 1)
                dve.wait_ge(st, s + 10)
                nc.vector.tensor_tensor(count[:, 0:e], count[:, 0:e], ps_rank[:, 16:16 + e], ALU.add).then_inc(st, 1)
                dve.wait_ge(st, s + 11)
                nc.vector.tensor_tensor(wgt[:, 1:2], wgt[:, 0:1], egap[:], ALU.mult).then_inc(st, 1)
                nc.vector.tensor_tensor(place[:, 0:e], place[:, 0:e], const("eoff")[:, 0:e], ALU.add).then_inc(st, 1)
                dve.wait_ge(st, s + 14)

                for c in range(2):
                    nc.vector.tensor_tensor_reduce(prod[:, 0:e], pick[:, c, 0:e], place[:, 0:e], 1.0, 0.0, ALU.mult, ALU.add,
                                                   slot_f[:, c:c + 1]).then_inc(slot_step[layer], 1)
                    dve.wait_ge(slot_step[layer], 3 * t + c + 1)
                nc.vector.tensor_copy(slot_i[:, slot], slot_f[:]).then_inc(slot_step[layer], 1)
                dve.wait_ge(slot_step[layer], 3 * t + 3)
                nc.vector.tensor_copy(entry[:, slot, :, 1].bitcast(F32), wgt[:]).then_inc(wgt_in[layer], 1)
                dve.wait_ge(wgt_in[layer], t + 1)
                nc.vector.tensor_copy(entry[:, slot, :, 0], tok_id[:, bass.ds(t, 1)].to_broadcast([P, 2])).then_inc(entry_ready[layer], 1)

            def attention(layer):
                def spread_queries(i):
                    wait(dve, sc_mm[layer], 2 * i)
                    for g in range(ACT_BLK[layer], HPC):
                        nc.vector.tensor_scalar(qblk[:, :, g], q_sb[:].rearrange("p c (b n) -> p (c b) n", n=16), const("block")[:, g:g + 1], None, ALU.mult).then_inc(qblk_ready[layer], 1)

                def step(i, d):
                    second, first = [], []
                    if live(i, 3):
                        wait(dve, proj_mm[layer], i - 2)
                        wait(dve, hb_ready[layer], i - 2)
                        hh = h[:, (d - 3) % UNROLL]
                        nc.vector.tensor_tensor(hh, ps_proj, hh, ALU.add).then_inc(h2_ready[layer], 1)
                        wait(dve, h2_ready[layer], i - 2)
                        if layer == 0 or not live(i, 0):
                            wait(dve, turned_mm[layer], i - 1)
                        second = [(hh, xln2[:, (d - 3) % 2], 1, ln2_step[layer], rstd2_ready[layer], i - 3)]
                    if live(i, 0):
                        first = [(h[:, d], xln[:], 0, ln_step[layer], rstd_ready[layer], i)]
                        if layer == 0:
                            if second:
                                layer_norms(*second)
                                second = []
                            wait(dve, tok_mm, i + 1)
                            wait_turn(dve, h2_out[0], i, d, 4)
                            wait(dve, ln2_step[0], LN_STEPS * (i - 3))
                            nc.vector.tensor_tensor(h[:, d], ps_tok, pos, ALU.add).then_inc(h_ready[0], 1)
                            dve.wait_ge(h_ready[0], i + 1)
                        elif isinstance(i, int):
                            dve.wait_ge(h_in[d], 16 * (i // UNROLL + 1))
                        else:
                            dve.wait_ge(h_in[d], (i - d) * (16 // UNROLL) + 16)
                        wait(dve, turned_mm[layer], i)
                    layer_norms(*second, *first)
                    if live(i, 1):
                        softmax(layer, i - 1, lambda: entries(layer, i - 4, d) if live(i, 4) else None)
                    elif live(i, 4):
                        entries(layer, i - 4, d)
                    if live(i, 3):
                        route(layer, i - 3)
                    if live(i, 0) and layer == 0:
                        wait(dve, qk_ready[0], 4 * i + 2)
                        spread_queries(i)
                    if live(i, 0) and layer == 1:
                        for part in range(2):
                            wait(dve, cos_ready, 2 * i + part + 1)
                            wait(dve, swap_mm, i + 1)
                            nc.vector.tensor_tensor(in_heads(qk_raw, part), ps_swap[:, part * D:(part + 1) * D].rearrange("p (b n) -> p b n", n=NPATCH),
                                                    rotary("sin"), ALU.mult).then_inc(rot_ready, 1)
                            wait(dve, rot_ready, 2 * i + part + 1)
                            wait(dve, sc_mm[1], 2 * i)
                            to = q_sb[:] if part == 0 else k_sb[:, :, 0:P]
                            nc.vector.tensor_tensor(to, rot[:, 2 * part:2 * part + 2], qk_raw[:, 2 * part:2 * part + 2], ALU.add).then_inc(rope_done, 1)
                        wait(dve, rope_done, 2 * i + 1)
                        spread_queries(i)
                    if live(i, 0):
                        if isinstance(i, int) and i == 0:
                            dve.wait_ge(small_in[layer], SMALL + 16 * (1 - layer))
                        wait(dve, v_mm[layer], i + 1)
                        wait(dve, o_mm[layer], 2 * (i - 1))
                        nc.vector.tensor_tensor(v_sb[:, d % 2, 0:D], ps_v, bias_v[:], ALU.add).then_inc(v_ready[layer], 1)
                    wait_turn(dve, xln2_out[layer], i, d, 4)
                steps(dve, step)

            def tile_table(layer):
                e, n, st = E[layer], NTILE[layer], tt_step[layer]
                dve.wait_ge(slot_step[layer], 3 * NT)
                cnt = count[0:1, 0:e]
                row = lambda name, m: const(name)[0:1, 0:m]
                nc.vector.tensor_tensor(tt_n[:, 0:e], cnt.unsqueeze(2).to_broadcast([1, e, 16]), row("steps", 16).unsqueeze(1).to_broadcast([1, e, 16]), ALU.is_gt).then_inc(st, 1)
                dve.wait_ge(st, 1)
                nc.vector.tensor_reduce(tt_tiles[:, 0:e], tt_n[:, 0:e], AX.X, ALU.add).then_inc(st, 1)
                dve.wait_ge(st, 2)
                tri = row("tri", 81).rearrange("p (x y) -> p x y", y=9)[:, 0:e, 0:e]
                nc.vector.tensor_tensor(tt_tri[:, 0:e, 0:e], tt_tiles[:, 0:e].unsqueeze(1).to_broadcast([1, e, e]), tri, ALU.mult).then_inc(st, 1)
                dve.wait_ge(st, 3)
                nc.vector.tensor_reduce(tt_end[:, 0:e], tt_tri[:, 0:e, 0:e], AX.X, ALU.add).then_inc(st, 1)
                dve.wait_ge(st, 4)
                nc.vector.tensor_tensor(tt_ge[:, 0:n, 0:e], row("tile", n).unsqueeze(2).to_broadcast([1, n, e]), tt_end[:, 0:e].unsqueeze(1).to_broadcast([1, n, e]), ALU.is_ge).then_inc(st, 1)
                dve.wait_ge(st, 5)
                nc.vector.tensor_reduce(tt_e[:, 0:n], tt_ge[:, 0:n, 0:e], AX.X, ALU.add).then_inc(st, 1)
                nc.vector.tensor_tensor(tt_gt[:, 0:n, 0:e], tt_ge[:, 0:n, 0:e], tt_tiles[:, 0:e].unsqueeze(1).to_broadcast([1, n, e]), ALU.mult).then_inc(st, 1)
                dve.wait_ge(st, 7)
                nc.vector.tensor_reduce(tt_s[:, 0:n], tt_gt[:, 0:n, 0:e], AX.X, ALU.add).then_inc(st, 1)
                nc.vector.tensor_scalar(tile_exp[:, 0:n], tt_e[:, 0:n], float(e - 1), None, ALU.min).then_inc(st, 1)
                dve.wait_ge(st, 8)
                nc.vector.tensor_tensor(tt_r[:, 0:n], row("tile", n), tt_s[:, 0:n], ALU.subtract).then_inc(st, 1)
                dve.wait_ge(st, 10)
                nc.vector.scalar_tensor_tensor(tt_r2[:, 0:n], tt_e[:, 0:n], float(TOK // P), tt_r[:, 0:n], ALU.mult, ALU.add).then_inc(tt_sum[layer], 1)
                dve.wait_ge(tt_sum[layer], 1)
                nc.vector.tensor_scalar(tile_row[:, 0:n], tt_r2[:, 0:n], float(P), None, ALU.mult).then_inc(st, 1)

            def moe(layer):
                n, hid = NTILE[layer], HID[layer]
                half = hid // 2
                dve.wait_ge(tt_step[layer], TT_STEPS)
                if layer == 1:
                    nc.vector.memset(act[:, hid:HPAD[1]], 0.0).then_inc(act_pad, 1)
                else:
                    dve.wait_ge(experts_in[0], W_DMAS[0])

                def bias(e, at, m):
                    return experts[:, bass.ds(e * SLOT + 3072 + at, m)]

                def hidden(j, e):
                    if layer == 0:
                        dve.wait_ge(g_mm[0], j + 1)
                        wait(dve, silu_ready[0], j)
                        nc.vector.tensor_tensor(gate_in, ps_g[:, 0], bias(e, 512, 512), ALU.add).then_inc(gbias_ready[0], 1)
                        dve.wait_ge(u_mm[0], j + 1)
                        nc.vector.tensor_tensor(up_in, ps_u[:, 0], bias(e, 0, 512), ALU.add).then_inc(ubias_ready[0], 1)
                        dve.wait_ge(ubias_ready[0], j + 1)
                        dve.wait_ge(silu_ready[0], j + 1)
                        nc.vector.tensor_tensor(act[:, 0:hid], up_in, gated[:, 0:hid], ALU.mult).then_inc(act_ready[0], 1)
                    else:
                        dve.wait_ge(u_mm[1], j + 1)
                        dve.wait_ge(silu_ready[1], j + 1)
                        nc.vector.tensor_tensor(act[:, 0:hid].rearrange("p (s n) -> p s n", s=2), ps_u[:, :, 0:half],
                                                gated[:, 0:hid].rearrange("p (s n) -> p s n", s=2), ALU.mult).then_inc(act_ready[1], 1)

                def weighted(j, e):
                    dve.wait_ge(y_mm[layer], j + 1)
                    wait(dve, added[layer], 16 * j)
                    w = places[:, bass.ds(j, 1), 1].bitcast(F32)
                    if layer == 0:
                        nc.vector.tensor_tensor(y_sb, ps_y[:, 0:D], bias(e, 1024, D), ALU.add).then_inc(yb_ready[0], 1)
                        dve.wait_ge(yb_ready[0], j + 1)
                        nc.vector.tensor_scalar(y_sb, y_sb, w, None, ALU.mult).then_inc(y_ready[0], 1)
                    else:
                        nc.vector.tensor_scalar(y_sb, ps_y[:, 0:D], w, None, ALU.mult).then_inc(y_ready[1], 1)

                load, now, before = expert_registers(dve, layer)
                hidden(0, now())
                load(1)

                def tile(j):
                    e, e_before = now(), before()
                    hidden(j, e)
                    load(j + 1)
                    weighted(j - 1, e_before)

                tile(1)
                with dve.Fori(2, n - 1) as j:
                    tile(j)
                last, e_before = now(), before()
                hidden(n - 1, last)
                weighted(n - 2, e_before)
                weighted(n - 1, last)

            dve.wait_ge(consts_in, N_CONST)
            dve.wait_ge(cast_done, 3)
            dve.wait_ge(pos_done, 1)
            for layer in range(2):
                nc.vector.memset(count[:], 0.0).then_inc(count_zero, 1)
                dve.wait_ge(count_zero, layer + 1)
                attention(layer)
                tile_table(layer)
                moe(layer)

        @block.tensor
        def _(pe):
            ident = const("ident")

            def attention(layer):
                def attend_first(i, d):
                    wait(pe, pblk_ready[layer], BLK * (i - 1))
                    wait(pe, v_ready[layer], i - 1)
                    wait(pe, oT_ready[layer], i - 2)
                    attend(0, 8, d).then_inc(o_mm[layer], 1)

                def values(k):
                    return nc.tensor.matmul(ps_v, xlnT[:, k], w_qkv[:, k, 2 * D:3 * D], start=k == 0, stop=k == KD - 1)

                def attend(lo, hi, d):
                    for g in range(lo, hi):
                        mm = nc.tensor.matmul(ps_o[:, g // 8, (g % 8) * WIN:(g % 8 + 1) * WIN],
                                              pblk[:, g].rearrange("p b n -> p (b n)"),
                                              v_sb[:, d % 2, g * HD:g * HD + WIN], start=True, stop=True)
                    return mm

                def step(i, d):
                    if layer == 0 and live(i, 0):
                        if isinstance(i, int):
                            pe.wait_ge(patch_in[d % 2], 16 * (i // 2 + 1))
                        else:
                            pe.wait_ge(patch_in[d % 2], (i - d) * 8 + 16 * (d // 2 + 1))
                        wait(pe, v_ready[0], i)
                        for k in range(KF):
                            mm = nc.tensor.matmul(ps_tok, patch[:, d % 2, k], w_tok[:, k], start=k == 0, stop=k == KF - 1)
                        mm.then_inc(tok_mm, 1)
                    if live(i, 1):
                        wait(pe, qblk_ready[layer], BLK * i)
                        wait(pe, qk_ready[layer], 4 * i)
                        if layer == 1:
                            wait(pe, rope_done, 2 * i)
                        for c in range(KD):
                            if c == 1:
                                wait(pe, h2_ready[layer], i - 2)
                            for b in range(IPT):
                                mm = nc.tensor.matmul(ps_sc[:, c, b * WIN:(b + 1) * WIN], qblk[:, c * IPT + b].rearrange("p g n -> p (g n)"),
                                                      k_sb[:, c, b * 16:b * 16 + WIN], start=True, stop=True)
                            mm.then_inc(sc_mm[layer], 1)
                    last = isinstance(i, int) and i == NT + 1
                    if last:
                        attend_first(i, d)
                        attend(8, 16, d).then_inc(o_mm[layer], 1)
                    if live(i, 4):
                        e = E[layer]
                        wait(pe, rt_step[layer], RT_STEPS * (i - 4) + 8)
                        wait(pe, pblk_ready[layer], BLK * min(i - 1, NT) if isinstance(i, int) else BLK * (i - 1))
                        if layer == 1:
                            wait(pe, rot_ready, 2 * min(i, NT) if isinstance(i, int) else 2 * i)
                        nc.tensor.matmul(ps_rank[:, 0:e], upper_bf[:], both_bf[:, 0:e], start=True, stop=True)
                        mm = nc.tensor.matmul(ps_rank[:, 16:16 + e], ones_bf[:], both_bf[:, 0:e], start=True, stop=True)
                        mm.then_inc(rank_mm[layer], 1)
                    if live(i, 0) or live(i, 3):
                        wait(pe, turned_ready[layer], i)
                        if live(i, 0):
                            wait(pe, ln_step[layer], LN_STEPS * (i + 1))
                            for c in range(KD):
                                mm = nc.tensor.transpose(ps_xT[:, c * P:(c + 1) * P], xln[:, c * P:(c + 1) * P], ident)
                        if live(i, 3):
                            wait(pe, ln2_step[layer], LN_STEPS * (i - 2))
                            for c in range(KD):
                                mm = nc.tensor.transpose(ps_x2T[:, c * P:(c + 1) * P], xln2[:, (d - 3) % 2, c * P:(c + 1) * P], ident)
                        mm.then_inc(turned_mm[layer], 1)
                    if live(i, 2) and not last:
                        attend_first(i, d)
                    if live(i, 3):
                        wait(pe, turned_ready[layer], i + 1)
                        wait(pe, o_ready[layer], 2 * (i - 2))
                        if isinstance(i, int) and i >= NT:
                            wait(pe, qk_ready[layer], 4 * NT)
                            wait(pe, rt_step[layer], RT_STEPS * (i - 4) + 1)
                        e = E[layer]
                        for k in range(KD):
                            mm = nc.tensor.matmul(ps_route(i - 3)[:, 0:e], xln2T[:, k], w_gate[:, k, 0:e], start=k == 0, stop=k == KD - 1)
                        mm.then_inc(route_mm[layer], 1)
                    if live(i, 0):
                        if isinstance(i, int) and i == 0:
                            pe.wait_ge(small_in[layer], SMALL + 16 * (1 - layer))
                        wait(pe, turned_ready[layer], i + 1)
                        wait(pe, qk_ready[layer], 4 * i)
                        for c in range(4):
                            for k in range(KD):
                                mm = nc.tensor.matmul(ps_qk[:, c * P:(c + 1) * P], w_qkv[:, k, c * P:(c + 1) * P], xlnT[:, k],
                                                      start=k == 0, stop=k == KD - 1)
                        mm.then_inc(qk_mm[layer], 1)
                    if live(i, 2) and not last:
                        if not isinstance(i, int) or i < NT:
                            wait(pe, rt_step[layer], RT_STEPS * (i - 3) + 1)
                        attend(8, 12, d)
                    if layer == 1 and live(i, 0):
                        wait(pe, rot_ready, 2 * i)
                        wait(pe, rt_step[1], RT_STEPS * (i - 4) + 12)
                        wait(pe, pblk_ready[1], BLK * (i - 1))
                        for c in range(4):
                            wait(pe, qk_ready[1], 4 * i + c + 1)
                            mm = nc.tensor.matmul(ps_swap[:, c * P:(c + 1) * P], const("swap"), qk_raw[:, c], start=True, stop=True)
                        mm.then_inc(swap_mm, 1)
                    if live(i, 2) and not last:
                        attend(12, 16, d).then_inc(o_mm[layer], 1)
                    if live(i, 0):
                        wait(pe, v_ready[layer], i)
                        values(0)
                    if live(i, 2):
                        wait(pe, o_ready[layer], 2 * (i - 1))
                        for c in range(KD):
                            mm = nc.tensor.transpose(ps_oT[:, c * P:(c + 1) * P], o_sb[:, c * P:(c + 1) * P], ident)
                        mm.then_inc(oT_mm[layer], 1)
                    if live(i, 1):
                        wait(pe, p_ready[layer], i)
                        wait(pe, rt_step[layer], RT_STEPS * (i - 4) + 12)
                        if layer == 1:
                            wait(pe, rot_ready, 2 * min(i + 1, NT) if isinstance(i, int) else 2 * (i + 1))
                        for c in range(2):
                            mm = nc.tensor.transpose(ps_pT[:, c * P:(c + 1) * P],
                                                     p_sb[:, c * IPT:(c + 1) * IPT].rearrange("p b k -> p (b k)"), ident)
                        mm.then_inc(pT_mm[layer], 1)
                    if live(i, 0):
                        values(1).then_inc(v_mm[layer], 1)
                    if live(i, 2):
                        wait(pe, oT_ready[layer], i - 1)
                        for k in range(KD):
                            mm = nc.tensor.matmul(ps_proj, oT[:, k], w_proj[:, k], start=k == 0, stop=k == KD - 1)
                        mm.then_inc(proj_mm[layer], 1)
                steps(pe, step)

            def moe(layer):
                n, hid = NTILE[layer], HID[layer]
                chunks = HPAD[layer] // P
                parts = 1 if layer == 0 else 2
                width = hid // parts
                at_g, at_u, at_d = (KD * hid, 0, 2 * KD * hid) if layer == 0 else (0, KD * hid, 2 * KD * hid)

                def turn_in(j):
                    pe.wait_ge(gather_in[layer], 16 * j + 16)
                    wait(pe, gT_ready[layer], j)
                    for c in range(KD):
                        mm = nc.tensor.transpose(ps_gT[:, c * P:(c + 1) * P], xg[:, c * P:(c + 1) * P], ident)
                    mm.then_inc(gT_mm[layer], 1)

                def into(ps, at, e, done):
                    for s in range(parts):
                        for k in range(KD):
                            mm = nc.tensor.matmul(ps[:, s, 0:width], xgT[:, k],
                                                  experts[:, bass.ds(e * SLOT + at + k * hid + s * width, width)],
                                                  start=k == 0, stop=k == KD - 1)
                    mm.then_inc(done, 1)

                def gate(j, e):
                    pe.wait_ge(gT_ready[layer], j + 1)
                    wait(pe, gbias_ready[0] if layer == 0 else silu_ready[1], j)
                    into(ps_g, at_g, e, g_mm[layer])

                def up(j, e):
                    wait(pe, act_ready[layer], j)
                    into(ps_u, at_u, e, u_mm[layer])

                def turn_act(j):
                    pe.wait_ge(act_ready[layer], j + 1)
                    wait(pe, aT_ready[layer], parts * j)
                    for c in range(chunks):
                        mm = nc.tensor.transpose(ps_aT[c // 4][:, (c % 4) * P:(c % 4 + 1) * P], act[:, c * P:(c + 1) * P], ident)
                    mm.then_inc(aT_mm[layer], 1)

                def down(j, e):
                    pe.wait_ge(aT_ready[layer], parts * (j + 1))
                    wait(pe, yb_ready[0] if layer == 0 else y_ready[1], j)
                    for k in range(chunks):
                        mm = nc.tensor.matmul(ps_y[:, 0:D], actT[:, k], experts[:, bass.ds(e * SLOT + at_d + k * D, D)],
                                              start=k == 0, stop=k == chunks - 1)
                    mm.then_inc(y_mm[layer], 1)

                pe.wait_ge(experts_in[layer], W_DMAS[layer])
                pe.wait_ge(tt_step[layer], TT_STEPS)
                if layer == 1:
                    pe.wait_ge(act_pad, 1)
                    pe.wait_ge(w_pad, 1)
                load, now, before = expert_registers(pe, layer)
                turn_in(0)
                e = now()
                gate(0, e)
                up(0, e)
                load(1)
                turn_in(1)

                def tile(j):
                    e, e_before = now(), before()
                    gate(j, e)
                    turn_act(j - 1)
                    up(j, e)
                    load(j + 1)
                    turn_in(j + 1)
                    down(j - 1, e_before)

                tile(1)
                with pe.Fori(2, n - 1) as j:
                    tile(j)
                last, e_before = now(), before()
                gate(n - 1, last)
                turn_act(n - 2)
                up(n - 1, last)
                down(n - 2, e_before)
                turn_act(n - 1)
                down(n - 1, last)

            pe.wait_ge(consts_in, N_CONST)
            pe.wait_ge(tokw_in, 16)
            pe.wait_ge(cast_done, 3)
            pe.wait_ge(pad_done, 2)
            for layer in range(2):
                attention(layer)
                moe(layer)


def _constants(np):
    p = np.arange(P)
    c = np.zeros((P, NCONST), np.float32)

    def put(name, v):
        at, n = CONSTS[name]
        c[:, at:at + n] = np.asarray(v, np.float32).reshape(-1, n)

    put("ident", np.eye(P))
    put("swap", np.eye(P)[p ^ 1])
    put("upper", p[:, None] < p[None, :])
    put("ones", np.ones((P, P)))
    pos = np.arange(NPATCH)
    freq = (np.float32(10000.0) ** (-2.0 * np.arange(HD // 2, dtype=np.float32) / HD)).astype(np.float32)
    angle = pos.astype(np.float32)[None, :] * freq[(p % HD) // 2][:, None]
    put("cos", np.cos(angle))
    put("sin", np.sin(angle) * np.where(p % 2 == 0, -1.0, 1.0)[:, None])
    q = (p % 16)[:, None, None]
    head = np.arange(2)[None, :, None] * HPC + (p // 16)[:, None, None]
    k = pos[None, None, :]
    hidden = k > q
    put("mask0", np.where(hidden, -1e30, (k - q) * 0.5 ** (head + 1.0)).reshape(P, 32))
    put("mask1", np.where(hidden + 0 * head, -1e30, 0.0).reshape(P, 32))
    put("block", (p // 16)[:, None] == np.arange(8)[None, :])
    put("tokid", p[:, None] + P * np.arange(NT)[None, :])
    put("eoff", np.arange(9) * TOK)
    put("eidx", np.arange(9))
    put("steps", np.arange(16) * P)
    put("tri", np.arange(9)[:, None] >= np.arange(9)[None, :])
    put("tile", np.arange(JMAX))
    put("nhalf", -0.5)
    return c


def kernel(**inputs):
    import numpy as np
    import concourse.bacc as bacc
    from concourse.bass_utils import run_bass_kernel_spmd as run

    x = {name: np.asarray(v) for name, v in inputs.items()}

    def rows(w):
        return w.reshape(-1, P, w.shape[-1]).transpose(1, 0, 2)

    def experts(w):
        return w.reshape(w.shape[0], -1, P, w.shape[-1]).transpose(0, 2, 1, 3).reshape(w.shape[0] * P, -1)

    patches = x["x"].reshape(IMGS, 3, 4, 16, 4, 16).transpose(1, 3, 5, 0, 2, 4)
    patches = patches.reshape(KF, P, NT, P).transpose(2, 1, 0, 3).reshape(NT * P, KF * P)
    a = {
        "consts": _constants(np),
        "zeros": np.zeros((P, D), np.float32),
        "patches": patches,
        "w_tok": rows(x["L0_tok_W"].T),
        "b_tok": x["L0_tok_b"],
        "pos": np.tile(x["L0_tok_pos_emb"], (IPT, 1)),
        "w_gate0": rows(x["L0_ffn_gate_w"].T),
        "b_gate": x["L0_ffn_gate_b"],
        "w_gate1": rows(x["L1_ffn_Wr"]),
        "w_up0": experts(x["L0_ffn_w0"].transpose(0, 2, 1)),
        "w_gate_h0": experts(x["L0_ffn_w1"].transpose(0, 2, 1)),
        "w_down0": experts(x["L0_ffn_w2"].transpose(0, 2, 1)),
        "b_exp": np.concatenate([x["L0_ffn_b0"], x["L0_ffn_b1"], x["L0_ffn_b2"]], axis=1).reshape(-1),
        "w_gate_h1": experts(x["L1_ffn_Wg"]),
        "w_up1": experts(x["L1_ffn_Wu"]),
        "w_down1": x["L1_ffn_Wd"].reshape(-1, D),
    }
    for layer, w, b in ((0, "L0_attn_W_attn", "L0_attn_b_attn"), (1, "L1_attn_W_qkv", "L1_attn_b_qkv")):
        a[f"w_qkv{layer}"] = rows(x[w])
        a[f"b_qk{layer}"] = x[b][:2 * D].reshape(4, P).T
        a[f"b_v{layer}"] = x[b][2 * D:]
        a[f"w_proj{layer}"] = rows(x[f"L{layer}_attn_W_proj"])
        a[f"b_proj{layer}"] = x[f"L{layer}_attn_b_proj"]
    for layer in range(2):
        empty = np.zeros(((E[layer] + 1) * TOK, 2), np.int32)
        empty[:, 0] = DUMMY + np.arange(len(empty)) % P
        a[f"empty{layer}"] = empty

    nc = bacc.Bacc("TRN2", target_bir_lowering=False, num_devices=1)
    arrays, aps = {}, {}
    for name, v in a.items():
        v = np.ascontiguousarray(v)
        arrays[f"in_{name}"] = v
        aps[name] = nc.dram_tensor(f"in_{name}", v.shape, mybir.dt.from_np(v.dtype), kind="ExternalInput").ap()
    tables = {
        "resid": nc.dram_tensor("resid", (ROWS, D), F32, kind="Internal").ap(),
        "normed0": nc.dram_tensor("normed0", (ROWS, D), F32, kind="Internal").ap(),
        "normed1": nc.dram_tensor("normed1", (ROWS, D), F32, kind="Internal").ap(),
        "table0": nc.dram_tensor("table0", ((E[0] + 1) * TOK, 2), I32, kind="Internal").ap(),
        "table1": nc.dram_tensor("table1", ((E[1] + 1) * TOK, 2), I32, kind="Internal").ap(),
    }
    out = nc.dram_tensor("out_0", (ROWS, D), F32, kind="ExternalOutput").ap()
    tower(nc, aps, tables, out)
    r = run(nc, [arrays], core_ids=[0])
    return r.results[0]["out_0"][:TOK].reshape(IMGS, NPATCH, D)
```
